# Optimizing a Trainium2 kernel written in Bass

```python
import numpy as np
import jax
import jax.numpy as jnp

def _softmax(x, axis=-1):
    return jax.nn.softmax(x, axis=axis)

def _gelu(x):
    return jax.nn.gelu(x, approximate=True)

def _silu(x):
    return jax.nn.silu(x)

def _sigmoid(x):
    return jax.nn.sigmoid(x)

def _layernorm(x, axis=-1, eps=1e-05):
    m = jnp.mean(x, axis=axis, keepdims=True)
    v = jnp.var(x, axis=axis, keepdims=True)
    return (x - m) / jnp.sqrt(v + eps)

def _scatter_add(tgt, idx, src, axis=0):
    return tgt.at[idx].add(src)

def _segment_sum(src, seg, n):
    return jax.ops.segment_sum(src, seg, n)
kernel_name = 'mk_seq_postln_d1_jaxref_r8_bbe017'

def setup_inputs(seed: int=0):
    np.random.seed(seed)
    _w = jnp.asarray

    def _L0_attn_setup():
        import jax, jax.numpy as jnp
        import numpy as np
        B, L, D_IN, D_OUT, H = (4, 256, 128, 128, 16)
        DH = D_OUT // H
        EPS = 1e-06

        def _rmsnorm(x, w):
            var = jnp.mean(jnp.square(x), axis=-1, keepdims=True)
            return x * jax.lax.rsqrt(var + EPS) * w
        key = jax.random.key(seed)
        ks = jax.random.split(key, 12)
        s_in = 1.0 / np.sqrt(D_IN)
        s_out = 1.0 / np.sqrt(D_OUT)
        return {'x': jax.random.normal(ks[0], (B, L, D_IN), jnp.float32), 'Wq': jax.random.normal(ks[1], (D_OUT, D_IN), jnp.float32) * s_in, 'Wk': jax.random.normal(ks[2], (D_OUT, D_IN), jnp.float32) * s_in, 'Wv': jax.random.normal(ks[3], (D_OUT, D_IN), jnp.float32) * s_in, 'Wg': jax.random.normal(ks[4], (D_OUT, D_IN), jnp.float32) * s_in, 'Wb': jax.random.normal(ks[5], (D_OUT, D_IN), jnp.float32) * s_in, 'Wa': jax.random.normal(ks[6], (H, D_IN), jnp.float32) * s_in, 'dt_bias': jnp.ones((H,), jnp.float32), 'A_log': jnp.log(jax.random.uniform(ks[7], (H,), jnp.float32, 0.001, 16.0)), 'norm_w': jnp.ones((DH,), jnp.float32), 'Wo': jax.random.normal(ks[8], (D_OUT, D_OUT), jnp.float32) * s_out, 'bo': jnp.zeros((D_OUT,), jnp.float32)}
    _L0_attn_in = _L0_attn_setup()

    def _L0_ffn_setup():
        import jax, jax.numpy as jnp
        import numpy as np
        S, B, H, I, E = (64, 2, 128, 352, 8)
        key = jax.random.key(seed)
        ks = jax.random.split(key, 5)
        return {'hidden_states': jax.random.normal(ks[0], (S, B, H), dtype=jnp.float32), 'router_w': jax.random.normal(ks[1], (E, H), dtype=jnp.float32) * 0.02, 'gate_w': jax.random.normal(ks[2], (E, I, H), dtype=jnp.float32) * 0.02, 'up_w': jax.random.normal(ks[3], (E, I, H), dtype=jnp.float32) * 0.02, 'down_w': jax.random.normal(ks[4], (E, H, I), dtype=jnp.float32) * 0.02}
    _L0_ffn_in = _L0_ffn_setup()
    _d = {'L0_attn_x': _L0_attn_in['x'], 'L0_attn_Wq': _L0_attn_in['Wq'], 'L0_attn_Wk': _L0_attn_in['Wk'], 'L0_attn_Wv': _L0_attn_in['Wv'], 'L0_attn_Wg': _L0_attn_in['Wg'], 'L0_attn_Wb': _L0_attn_in['Wb'], 'L0_attn_Wa': _L0_attn_in['Wa'], 'L0_attn_dt_bias': _L0_attn_in['dt_bias'], 'L0_attn_A_log': _L0_attn_in['A_log'], 'L0_attn_norm_w': _L0_attn_in['norm_w'], 'L0_attn_Wo': _L0_attn_in['Wo'], 'L0_attn_bo': _L0_attn_in['bo'], 'L0_ffn_router_w': _L0_ffn_in['router_w'], 'L0_ffn_gate_w': _L0_ffn_in['gate_w'], 'L0_ffn_up_w': _L0_ffn_in['up_w'], 'L0_ffn_down_w': _L0_ffn_in['down_w']}
    _x0 = _d['L0_attn_x']
    _d['L0_attn_x'] = jax.random.normal(jax.random.fold_in(jax.random.key(seed), 1), (16, 512, 128), dtype=_x0.dtype)
    del _x0
    return _d

def reference(L0_attn_x, L0_attn_Wq, L0_attn_Wk, L0_attn_Wv, L0_attn_Wg, L0_attn_Wb, L0_attn_Wa, L0_attn_dt_bias, L0_attn_A_log, L0_attn_norm_w, L0_attn_Wo, L0_attn_bo, L0_ffn_router_w, L0_ffn_gate_w, L0_ffn_up_w, L0_ffn_down_w):

    def _L0_attn_ref(x, Wq, Wk, Wv, Wg, Wb, Wa, dt_bias, A_log, norm_w, Wo, bo):
        import jax, jax.numpy as jnp
        import numpy as np
        B, L, D_IN, D_OUT, H = (4, 256, 128, 128, 16)
        DH = D_OUT // H
        EPS = 1e-06

        def _rmsnorm(x, w):
            var = jnp.mean(jnp.square(x), axis=-1, keepdims=True)
            return x * jax.lax.rsqrt(var + EPS) * w
        b, l, _ = x.shape
        q = (x @ Wq.T).reshape(b, l, H, DH)
        k = (x @ Wk.T).reshape(b, l, H, DH)
        v = (x @ Wv.T).reshape(b, l, H, DH)
        gate = (x @ Wg.T).reshape(b, l, H, DH)
        beta = jax.nn.sigmoid(x @ Wb.T).reshape(b, l, H, DH)
        alpha = jnp.exp(-jnp.exp(A_log)[None, None, :] * jax.nn.softplus(x @ Wa.T + dt_bias))
        q = q / jnp.linalg.norm(q, axis=-1, keepdims=True) / np.sqrt(DH)
        k = k / jnp.linalg.norm(k, axis=-1, keepdims=True)

        def step(S, inp):
            k_t, q_t, v_t, beta_t, a_t = inp
            S = S * a_t[..., None, None]
            kv_mem = jnp.einsum('bhd,bhde->bhe', k_t, S)
            delta = (v_t - kv_mem) * beta_t
            S = S + k_t[..., :, None] * delta[..., None, :]
            y_t = jnp.einsum('bhd,bhde->bhe', q_t, S)
            return (S, y_t)
        tfirst = lambda a: jnp.moveaxis(a, 1, 0)
        S0 = jnp.zeros((b, H, DH, DH), x.dtype)
        _, ys = jax.lax.scan(step, S0, (tfirst(k), tfirst(q), tfirst(v), tfirst(beta), tfirst(alpha)))
        ys = jnp.moveaxis(ys, 0, 1)
        ctx = _rmsnorm(ys, norm_w) * jax.nn.silu(gate)
        ctx = ctx.reshape(b, l, D_OUT)
        return ctx @ Wo.T + bo

    def _L0_ffn_ref(hidden_states, router_w, gate_w, up_w, down_w):
        import jax, jax.numpy as jnp
        import numpy as np
        S, B, H, I, E = (64, 2, 128, 352, 8)
        router_logits = jnp.einsum('sbh,eh->sbe', hidden_states, router_w)
        routing_indices = jnp.argmax(router_logits, axis=-1)
        out = jnp.zeros_like(hidden_states)
        for e in range(E):
            mask = (routing_indices == e)[..., None]
            xe = jnp.where(mask, hidden_states, 0.0)
            g = jnp.einsum('sbh,ih->sbi', xe, gate_w[e])
            u = jnp.einsum('sbh,ih->sbi', xe, up_w[e])
            ye = jnp.einsum('sbi,hi->sbh', jax.nn.silu(g) * u, down_w[e])
            out = out + jnp.where(mask, ye, 0.0)
        return out
    x = L0_attn_x
    x = _layernorm(x + _L0_attn_ref(x, L0_attn_Wq, L0_attn_Wk, L0_attn_Wv, L0_attn_Wg, L0_attn_Wb, L0_attn_Wa, L0_attn_dt_bias, L0_attn_A_log, L0_attn_norm_w, L0_attn_Wo, L0_attn_bo), axis=-1)
    x = _layernorm(x + _L0_ffn_ref(x, L0_ffn_router_w, L0_ffn_gate_w, L0_ffn_up_w, L0_ffn_down_w), axis=-1)
    return x

_drawn_inputs = setup_inputs


def setup_inputs(seed=0):
    import zlib

    import numpy as np

    out = dict(_drawn_inputs(seed))
    spreads = {'L0_attn_dt_bias': (1.0, 0.6), 'L0_attn_norm_w': (1.0, 0.2), 'L0_attn_bo': (0.0, 0.1)}
    factors = {'L0_ffn_router_w': 6.232,
     'L0_ffn_gate_w': 5.903,
     'L0_ffn_up_w': 5.862,
     'L0_ffn_down_w': 5.863}
    for name, (base, spread) in spreads.items():
        noise = np.random.default_rng([zlib.crc32(name.encode()), seed]).standard_normal(out[name].shape)
        drawn = base * np.exp(spread * noise) if base else spread * noise
        out[name] = jnp.asarray(drawn.astype(out[name].dtype))
    for name, factor in factors.items():
        out[name] = (out[name] * factor).astype(out[name].dtype)
    return out
```

```python
from contextlib import ExitStack

import concourse.bass as bass
from concourse import mybir

F32 = mybir.dt.float32
I32 = mybir.dt.int32
ALU = mybir.AluOpType
ACT = mybir.ActivationFunctionType
AX = mybir.AxisListType.X

P = 128
NB, L, D = 16, 512, 128
H, DH = 16, 8
T, C = 32, 4
NW, NCH = L // T, T // C
WN = NB * T
NN = NB * NCH
TW = WN // P
NT = NW * TW
E, I = 8, 352
IC = (I + P - 1) // P
MT = NT + E
LN_EPS, RMS_EPS = 1e-5, 1e-6

PRE_ONLY, FIRST, FULL, LAST, POST_ONLY = range(5)
HAS_PRE = (True, True, True, False, False)
HAS_CHAIN = (False, True, True, True, False)
HAS_POST = (False, False, True, True, True)


class Win:

    def __init__(self, i, par):
        self.i, self.par = i, par

    @property
    def w(self):
        return self.i * 2 + self.par

    def shift(self, n):
        return Win(self.i + (self.par + n) // 2, (self.par + n) % 2)


class Steps:

    def __init__(self, sem):
        self.sem, self.order, self.kind = sem, {}, None

    def count(self, kind):
        return len(self.order[kind])

    def value(self, label, kind, body):
        at = self.order[kind].index(label) + 1
        if kind == PRE_ONLY:
            return at
        at = at + self.count(PRE_ONLY)
        if kind == FIRST:
            return at
        at = at + self.count(FIRST)
        if kind == POST_ONLY:
            return at + (NW - 2) * self.count(FULL) + self.count(LAST)
        return (body - 1) * self.count(FULL) + at


def kind_of(win, first, last):
    return FIRST if first else LAST if last else FULL


def upd_prod(upd):
    flat = upd[:, :, :, :].rearrange("p b d s -> p (b d s)")
    return flat[:, 0:C * NB * DH].rearrange("p (j b d) -> p j b d", j=C, b=NB)


def block_kernel(nc, t):
    ctx = ExitStack()
    with ctx:
        def sb(name, shape, dt=F32):
            return ctx.enter_context(nc.sbuf_tensor(name, shape, dt))

        def sem(name):
            return ctx.enter_context(nc.semaphore(name))

        def two(name, shape):
            return [sb(f"{name}{n}", shape) for n in range(2)]

        w_proj = sb("w_proj", [P, 6, D])
        w_a = sb("w_a", [P, H])
        w_o = sb("w_o", [P, D])
        w_r = sb("w_r", [P, E])
        ident = sb("ident", [P, P])
        heads = sb("heads", [P, P])
        heads_mean = sb("heads_mean", [P, P])
        below = sb("below", [P, P])
        ones = sb("ones", [P, P])
        bias_o = sb("bias_o", [1, WN])
        iota_e = sb("iota_e", [P, E])
        iota_t = sb("iota_t", [1, MT])
        dt_b = sb("dt_b", [P, 1])
        neg_a = sb("neg_a", [P, 1])
        norm_w = sb("norm_w", [P, 1])
        q_bias = sb("q_bias", [P, 1])
        rms_eps = sb("rms_eps", [P, 1])
        ln_eps = sb("ln_eps", [P, 1])
        zero = sb("zero", [P, D])
        x1_all = sb("x1_all", [P, NT, D])
        logits = sb("logits", [P, NT, E])
        stats = sb("stats", [P, TW, 6])
        mv = sb("mv", [P, TW, 2])
        rstd = sb("rstd", [P, TW])

        att = ExitStack()
        att.__enter__()

        def sa(name, shape):
            return att.enter_context(nc.sbuf_tensor(name, shape, F32))

        def two_a(name, shape):
            return [sa(f"{name}{n}", shape) for n in range(2)]

        x_ct = two_a("x_ct", [P, WN])
        x_tc = sa("x_tc", [P, TW * D])
        k_rep = two_a("k_rep", [P, DH, WN])
        q_rep = two_a("q_rep", [P, DH, WN])
        beta_v = two_a("beta_v", [P, WN])
        beta_gam = two_a("beta_gam", [P, WN])
        gam = two_a("gam", [P, WN])
        to_end = two_a("to_end", [P, C, NN])
        akk = two_a("akk", [P, 9, NN])
        aqk = two_a("aqk", [P, 10, NN])
        delta = two_a("delta", [P, C, NN])
        gate = two_a("gate", [P, WN])
        z_r, z_a = sa("z_r", [P, WN]), sa("z_a", [P, WN])
        b_r, b_a = sa("b_r", [P, WN]), sa("b_a", [P, WN])
        g_r, g_a = z_r, b_a
        alpha, beta = sa("alpha", [P, WN]), sa("beta", [P, WN])
        k_s, q_s = sa("k_s", [P, WN]), sa("q_s", [P, WN])
        k_sq, q_sq = sa("k_sq", [P, WN]), sa("q_sq", [P, WN])
        far = sa("far", [P, 3, NN])
        beta_near = sa("beta_near", [P, 3, NN])
        beta_far = sa("beta_far", [P, 3, NN])
        kk = sa("kk", [P, 6, NN])
        qk = sa("qk", [P, 10, NN])
        S = two_a("S", [P, NB, DH])
        ks = sa("ks", [P, C, NB])
        tri = sa("tri", [P, C - 1, NB])
        d_end = sa("d_end", [P, C, NB])
        upd = sa("upd", [P, NB, DH, C + 1])
        prod = upd_prod(upd)
        q_prod = two_a("q_prod", [P, DH, C, NB])
        y_prod = qk
        y_sq = sa("y_sq", [P, WN])
        x1 = sa("x1", [P, TW, D])
        y_n = x1[:, :, :].rearrange("p i n -> p (i n)")
        ctx_t = sa("ctx_t", [P, WN])
        x1_ct = y_sq[:, :].rearrange("p (i n) -> p i n", i=TW)

        pb = [ctx.enter_context(nc.psum_tensor(f"bank{n}", [P, WN], F32)) for n in range(8)]
        ring, y_ps, post_ps = pb[0:4], pb[4:6], pb[6:8]

        s_const = sem("s_const")
        s_setup = sem("s_setup")
        s_zero = sem("s_zero")
        s_xct = [sem(f"s_xct{n}") for n in range(2)]
        s_xtc = [sem(f"s_xtc{n}") for n in range(2)]
        s_kout, s_qout = sem("s_kout"), sem("s_qout")
        s_krep, s_qrep = ([sem(f"s_{n}rep{m}") for m in range(2)] for n in "kq")
        act, dve, pool, pe = (Steps(sem(f"s_{n}")) for n in ("act", "dve", "pool", "pe"))

        att.close()
        U = 4
        gate_we = sb("gate_we", [P, E, I])
        up_we = sb("up_we", [P, E, I])
        down_we = sb("down_we", [P, IC, E, D])
        top = sb("top", [P, NT])
        cand = sb("cand", [P, NT, E])
        one_hot = sb("one_hot", [P, NT, E])
        total = sb("total", [P, NT, E])
        before = sb("before", [P, NT, E])
        tiles_i = sb("tiles_i", [P, E], I32)
        tiles_f = sb("tiles_f", [P, E])
        tile_end = sb("tile_end", [P, E])
        settle = sb("settle", [P, 1])
        place_f = sb("place_f", [P, NT])
        place = sb("place", [P, NT], I32)
        past = sb("past", [1, MT, E])
        expert_f = sb("expert_f", [1, MT])
        expert_at = sb("expert_at", [1, MT], I32)
        xs = [sb(f"xs{n}", [P, D]) for n in range(U)]
        ys = [sb(f"ys{n}", [P, D]) for n in range(U)]
        xs_t = two("xs_t", [P, P])
        silu = two("silu", [P, I])
        hid = two("hid", [P, IC * P])
        hid_t = two("hid_t", [P, IC, P])
        back_y = two("back_y", [P, TW, D])
        res_y = two("res_y", [P, TW, D])
        out_y = two("out_y", [P, TW, D])

        s_wexp = sem("s_wexp")
        s_route, s_count, s_pad = sem("s_route"), sem("s_count"), sem("s_pad")
        s_sorted, s_back = sem("s_sorted"), [sem(f"s_back{n}") for n in range(2)]
        s_xs, s_ys = ([sem(f"s_{m}{n}") for n in range(U)] for m in ("xs", "ys"))
        s_xturn, s_xt, s_up, s_silu, s_hid, s_hturn, s_ht, s_down, s_y = (
            sem(f"s_{n}") for n in ("xturn", "xt", "up", "silu", "hid", "hturn", "ht", "down", "y"))
        s_pad2, s_stat = sem("s_pad2"), sem("s_stat")
        s_sum, s_var, s_rstd, s_norm = (sem(f"s_{n}") for n in ("sum", "var", "rstd", "norm"))
        s_out = [sem(f"s_out{n}") for n in range(2)]
        turn_ps, hturn_ps, down_ps = pb[0], pb[1], pb[2]
        g_ps, u_ps = pb[3:5], pb[5:7]
        n_route = 0

        def attention_done(eng):
            for st, last in ((pe, "router"), (act, "x1_ct"), (pool, "ctx"), (dve, "logits")):
                eng.wait_ge(st.sem, st.value(last, POST_ONLY, NW))

        def route(eng):
            v, n = nc.vector, 0

            def link(ins):
                nonlocal n
                n += 1
                ins.then_inc(s_route, 1)
                eng.wait_ge(s_route, n)

            def over_t(x):
                return x.unsqueeze(2).to_broadcast([P, NT, E])

            def over_e(x):
                return x.unsqueeze(1).to_broadcast([P, NT, E])
            link(v.tensor_reduce(top[:, :], logits[:, :, :], AX, ALU.max))
            link(v.tensor_tensor(cand[:, :, :], logits[:, :, :], over_t(top[:, :]), ALU.is_equal))
            link(v.scalar_tensor_tensor(cand[:, :, :], cand[:, :, :], -float(E), over_e(iota_e[:, :]), ALU.mult, ALU.add))
            link(v.tensor_reduce(top[:, :], cand[:, :, :], AX, ALU.min))
            link(v.tensor_tensor(one_hot[:, :, :], cand[:, :, :], over_t(top[:, :]), ALU.is_equal))
            eng.wait_ge(s_count, 2)
            link(v.tensor_copy(total[:, :, :].rearrange("p t e -> p (t e)"), pb[1][:, 0:NT * E]))
            for e in range(E):
                link(v.tensor_tensor_scan(before[:, :, e], ones[:, 0:NT], total[:, :, e], 0.0, ALU.mult, ALU.add))
            link(v.tensor_scalar(tiles_f[:, :], before[:, NT - 1, :], float(P - 1), None, ALU.add))
            link(v.tensor_copy(tiles_i[:, :], tiles_f[:, :]))
            link(v.tensor_scalar(tiles_i[:, :], tiles_i[:, :], P.bit_length() - 1, None, ALU.logical_shift_right))
            link(v.tensor_copy(tiles_f[:, :], tiles_i[:, :]))
            link(v.tensor_tensor_scan(tile_end[:, :], ones[:, 0:E], tiles_f[:, :], 0.0, ALU.mult, ALU.add))
            link(v.tensor_tensor(tiles_f[:, :], tile_end[:, :], tiles_f[:, :], ALU.subtract))
            link(v.tensor_scalar(tiles_f[:, :], tiles_f[:, :], float(P), None, ALU.mult))
            link(v.tensor_tensor(before[:, :, :], before[:, :, :], total[:, :, :], ALU.subtract))
            link(v.tensor_tensor(before[:, :, :], before[:, :, :], over_e(tiles_f[:, :]), ALU.add))
            link(v.tensor_tensor(before[:, :, :], pb[0][:, 0:NT * E].rearrange("p (t e) -> p t e", e=E), before[:, :, :], ALU.add))
            link(v.tensor_tensor(before[:, :, :], before[:, :, :], one_hot[:, :, :], ALU.mult))
            link(v.tensor_reduce(place_f[:, :], before[:, :, :], AX, ALU.add))
            link(v.tensor_copy(place[:, :], place_f[:, :]))
            link(v.tensor_tensor(past[:, :, :], tile_end[0:1, :].unsqueeze(1).to_broadcast([1, MT, E]),
                                 iota_t[:, :].unsqueeze(2).to_broadcast([1, MT, E]), ALU.is_le))
            link(v.tensor_reduce(expert_f[:, :], past[:, :, :], AX, ALU.add))
            link(v.tensor_scalar(expert_f[:, :], expert_f[:, :], float(E - 1), None, ALU.min))
            link(v.tensor_copy(expert_at[:, :], expert_f[:, :]))
            return n

        n_route_hot, n_route_all = 5, 23 + E

        def sorted_tiles(eng, stage):
            for u in range(U):
                stage(0, u, True)
            with eng.Fori(1, MT // U - 1) as i:
                for u in range(U):
                    stage(i, u, True)
            for u in range(U):
                stage(MT // U - 1, u, u < U - 1)

        def token_windows(eng, stage):
            for par in range(2):
                stage(0, par)
            with eng.Fori(1, NW // 2) as i:
                for par in range(2):
                    stage(i, par)

        def at_least(eng, s, value):
            if not isinstance(value, int) or value > 0:
                eng.wait_ge(s, value)

        def finish_sync(eng):
            attention_done(eng)
            eng.dma_start(gate_we[:, :, :], t["gate_w"]).then_inc(s_wexp, 16)
            eng.dma_start(up_we[:, :, :], t["up_w"]).then_inc(s_wexp, 16)
            eng.dma_start(down_we[:, :, :, :], t["down_w"]).then_inc(s_wexp, 16)
            eng.wait_ge(s_sorted, 16 * NT)

            def load(tile, u):
                eng.dma_start(xs[u][:, :], t["x_sorted"][bass.ds(tile * P, P), :]).then_inc(s_xs[u], 16)
            for u in range(U):
                load(u, u)

            def stage(i, u, more):
                tile = i * U + u
                eng.wait_ge(s_y, tile + 1)
                eng.dma_start(t["y_sorted"][bass.ds(tile * P, P), :], ys[u][:, :]).then_inc(s_ys[u], 16)
                if not isinstance(i, int) or i == 0:
                    eng.wait_ge(s_xturn, tile + 1)
                    load(tile + U, u)
            sorted_tiles(eng, stage)

            def out(i, par):
                eng.wait_ge(s_norm, 4 * (i * 2 + par) + 4)
                eng.dma_start(t["out"][bass.ds(i * 2 + par, 1), :, :].rearrange("o p n -> (o p) n"),
                              out_y[par][:, :, :].rearrange("p i d -> p (i d)")).then_inc(s_out[par], 16)
            token_windows(eng, out)
            for par in range(2):
                eng.wait_ge(s_out[par], 16 * (NW // 2))

        def finish_pe(eng):
            attention_done(eng)
            mm, tr = nc.tensor.matmul, nc.tensor.transpose
            eng.wait_ge(s_route, n_route_hot)
            hot = one_hot[:, :, :].rearrange("p t e -> p (t e)")
            mm(pb[0][:, 0:NT * E], below[:, :], hot, start=True, stop=True).then_inc(s_count, 1)
            mm(pb[1][:, 0:NT * E], ones[:, :], hot, start=True, stop=True).then_inc(s_count, 1)
            eng.wait_ge(s_route, n_route_all)
            eng.wait_ge(s_wexp, 48)

            def x_turn(i, u):
                tile = i * U + u
                eng.wait_ge(s_xs[u], (i + 1) * 16)
                at_least(eng, s_xt, tile)
                tr(turn_ps[:, 0:P], xs[u][:, :], ident[:, :]).then_inc(s_xturn, 1)

            def gate_up(i, u):
                tile, par = i * U + u, u % 2
                at = eng.value_load(expert_at[0:1, bass.ds(tile, 1)], min_val=0, max_val=E - 1) * I
                eng.wait_ge(s_xt, tile + 1)
                at_least(eng, s_hid, tile - 1)
                for ps, we in ((g_ps, gate_we), (u_ps, up_we)):
                    mm(ps[par][:, 0:I], xs_t[par][:, :], we[:, :, :].rearrange("p e i -> p (e i)")[:, bass.ds(at, I)],
                       start=True, stop=True).then_inc(s_up, 1)

            def h_turn(i, u):
                tile, par = i * U + u, u % 2
                eng.wait_ge(s_hid, tile + 1)
                at_least(eng, s_ht, tile)
                for c in range(IC):
                    last = tr(hturn_ps[:, c * P:(c + 1) * P], hid[par][:, c * P:(c + 1) * P], ident[:, :])
                last.then_inc(s_hturn, 1)

            def down(i, u):
                tile, par = i * U + u, u % 2
                at = eng.value_load(expert_at[0:1, bass.ds(tile, 1)], min_val=0, max_val=E - 1) * D
                eng.wait_ge(s_ht, tile + 1)
                at_least(eng, s_y, tile)
                for c in range(IC):
                    last = mm(down_ps[:, 0:D], hid_t[par][:, c, :],
                              down_we[:, c, :, :].rearrange("p e d -> p (e d)")[:, bass.ds(at, D)],
                              start=(c == 0), stop=(c == IC - 1))
                last.then_inc(s_down, 1)

            def stage(i, u, more):
                j, w = (i, u + 1) if u < U - 1 else (i + 1, 0)
                if more:
                    x_turn(j, w)
                h_turn(i, u)
                if more:
                    gate_up(j, w)
                down(i, u)
            x_turn(0, 0)
            gate_up(0, 0)
            sorted_tiles(eng, stage)

        def finish_act(eng):
            attention_done(eng)
            A = nc.scalar.activation

            def x_copy(i, u):
                tile, par = i * U + u, u % 2
                eng.wait_ge(s_xturn, tile + 1)
                at_least(eng, s_up, 2 * tile - 2)
                A(xs_t[par][:, :], turn_ps[:, 0:P], ACT.Copy).then_inc(s_xt, 1)

            def silu_of(i, u):
                tile, par = i * U + u, u % 2
                eng.wait_ge(s_up, 2 * tile + 1)
                at_least(eng, s_hid, tile - 1)
                A(silu[par][:, :], g_ps[par][:, 0:I], ACT.Silu).then_inc(s_silu, 1)

            def h_copy(i, u):
                tile, par = i * U + u, u % 2
                eng.wait_ge(s_hturn, tile + 1)
                at_least(eng, s_down, tile - 1)
                A(hid_t[par][:, :, :].rearrange("p c n -> p (c n)"), hturn_ps[:, 0:IC * P], ACT.Copy).then_inc(s_ht, 1)

            def stage(i, u, more):
                j, w = (i, u + 1) if u < U - 1 else (i + 1, 0)
                if more:
                    x_copy(j, w)
                h_copy(i, u)
                if more:
                    silu_of(j, w)
            x_copy(0, 0)
            silu_of(0, 0)
            sorted_tiles(eng, stage)

            def norm(i, par):
                w = i * 2 + par
                eng.wait_ge(s_var, TW * (w + 1))
                A(rstd[:, :], mv[:, :, 1], ACT.Ln, bias=ln_eps[:, 0:1]).then_inc(s_rstd, 1)
                eng.wait_ge(s_rstd, 2 * w + 1)
                A(rstd[:, :], rstd[:, :], ACT.Exp, scale=-0.5).then_inc(s_rstd, 1)
            token_windows(eng, norm)

        def finish_pool(eng):
            attention_done(eng)
            eng.wait_ge(s_pad, 16)
            eng.wait_ge(s_route, n_route_all)

            def index(m):
                return bass.IndirectOffsetOnAxis(ap=place[:, m:m + 1], axis=0)
            for m in range(NT):
                eng.indirect_dma_start(t["x_sorted"], index(m), x1_all[:, m, :], None).then_inc(s_sorted, 16)
            for u in range(U):
                eng.wait_ge(s_ys[u], 16 * (MT // U))
            for w in range(NW):
                if w >= 2:
                    eng.wait_ge(s_sum, w - 1)
                for i in range(TW):
                    eng.indirect_dma_start(back_y[w % 2][:, i, :], None, t["y_sorted"], index(w * TW + i)) \
                        .then_inc(s_back[w % 2], 16)

        def finish_dve(eng):
            attention_done(eng)
            v = nc.vector
            assert route(eng) == n_route_all
            for par in range(2):
                v.memset(hid[par][:, I:IC * P], 0.0).then_inc(s_pad2, 1)
            eng.wait_ge(s_pad2, 2)

            def hidden(i, u):
                tile, par = i * U + u, u % 2
                eng.wait_ge(s_silu, tile + 1)
                eng.wait_ge(s_up, 2 * tile + 2)
                at_least(eng, s_hturn, tile - 1)
                v.tensor_tensor(hid[par][:, 0:I], u_ps[par][:, 0:I], silu[par][:, :], ALU.mult).then_inc(s_hid, 1)

            def y_copy(i, u):
                eng.wait_ge(s_down, i * U + u + 1)
                at_least(eng, s_ys[u], i * 16)
                v.tensor_copy(ys[u][:, :], down_ps[:, 0:D]).then_inc(s_y, 1)

            def stage(i, u, more):
                j, w = (i, u + 1) if u < U - 1 else (i + 1, 0)
                if more:
                    hidden(j, w)
                y_copy(i, u)
            hidden(0, 0)
            sorted_tiles(eng, stage)

            def norm(i, par):
                w = i * 2 + par
                eng.wait_ge(s_back[par], 16 * TW * (i + 1))
                v.tensor_tensor(res_y[par][:, :, :], back_y[par][:, :, :], x1_all[:, bass.ds(w * TW, TW), :], ALU.add) \
                    .then_inc(s_sum, 1)
                eng.wait_ge(s_sum, w + 1)
                for k in range(TW):
                    v.bn_stats(stats[:, k, :], res_y[par][:, k, :]).then_inc(s_stat, 1)
                eng.wait_ge(s_stat, TW * (w + 1))
                v.tensor_copy(settle[:, :], ones[:, 0:1])
                for k in range(TW):
                    v.bn_aggr(mv[:, k, :], stats[:, k, :]).then_inc(s_var, 1)
                eng.wait_ge(s_rstd, 2 * w + 2)
                at_least(eng, s_out[par], 16 * i)
                for k in range(TW):
                    v.tensor_scalar(out_y[par][:, k, :], res_y[par][:, k, :], mv[:, k, 0:1], rstd[:, k:k + 1],
                                    ALU.subtract, ALU.mult).then_inc(s_norm, 1)
                eng.wait_ge(s_norm, TW * (w + 1))
            token_windows(eng, norm)

        block = ctx.enter_context(nc.Block())

        def slots(tile):
            return tile[:, :].rearrange("p (n j) -> p j n", j=C)

        def chunk_jb(tile, c):
            return tile[:, :].rearrange("p (b c j) -> p c j b", c=NCH, j=C)[:, c, :, :]

        def slot_chunk(tile, c):
            return tile[:, :, :].rearrange("p s (b c) -> p c s b", c=NCH)[:, c, :, :]

        def rep_chunk(tile, c, order):
            return tile[:, :, :].rearrange("p d (b c j) -> p c d b j", c=NCH, j=C)[:, c, :, :, :] \
                .rearrange(f"p d b j -> p {order}")

        class Body:

            def __init__(self, steps, eng, kind, win, dry):
                self.steps, self.eng, self.kind, self.win, self.dry = steps, eng, kind, win, dry
                if dry:
                    steps.order[kind] = []
                self.at = 0

            def step(self, label, ins):
                if self.dry:
                    self.steps.order[self.kind].append(label)
                else:
                    assert self.steps.order[self.kind][self.at] == label
                    ins().then_inc(self.steps.sem, 1)
                self.at += 1

            def wait(self, steps, label, back=0):
                if self.dry:
                    return
                kind, body = self.kind, self.win.w
                if back:
                    n = body if isinstance(body, int) else None
                    if n is None:
                        kind = FULL
                    else:
                        m = n - back
                        kind = PRE_ONLY if m == -1 else FIRST if m == 0 else LAST if m == NW - 1 else FULL
                        if m < -1:
                            return
                if label not in steps.order[kind]:
                    return
                self.eng.wait_ge(steps.sem, steps.value(label, kind, body - back))

            def own(self):
                if self.dry or not self.at:
                    return
                label = self.steps.order[self.kind][self.at - 1]
                self.eng.wait_ge(self.steps.sem, self.steps.value(label, self.kind, self.win.w))

            def dma(self, sems, win, per=16):
                if not self.dry:
                    self.eng.wait_ge(sems[win.par], (win.i + 1) * per)

            def dma1(self, s, win, per=16):
                if not self.dry:
                    self.eng.wait_ge(s, (win.w + 1) * per)

        def pe_body(b):
            w = b.win
            pre, chain, post = HAS_PRE[b.kind], HAS_CHAIN[b.kind], HAS_POST[b.kind]
            nxt, prv = w.shift(1), w.shift(-1)
            mm, tr = nc.tensor.matmul, nc.tensor.transpose

            def project(label, n, bank, free_by, back=0):
                b.wait(*free_by, back=back)
                b.step(label, lambda: mm(ring[bank][:, :], w_proj[:, n, :], x_ct[nxt.par][:, :], start=True, stop=True))

            def head_sum(label, src, bank, ready, free_by):
                b.wait(*ready)
                b.wait(*free_by)
                b.step(label, lambda: mm(ring[bank][:, 0:src.shape[1]], heads[:, :], src, start=True, stop=True))

            def y_chunk(c):
                b.wait(pool, f"q_prod{c}")
                if c == 0:
                    b.wait(act, "y_sq", back=1)
                    b.wait(dve, "y_n", back=1)
                out = y_ps[w.par][:, :].rearrange("p (j b c) -> p c j b", j=C, c=NCH)[:, c, :, :]

                def go():
                    for d in range(DH):
                        i = mm(out, ident[:, :], q_prod[c % 2][:, d, :, :], start=(c == 0 and d == 0), stop=(d == DH - 1),
                               skip_group_check=True)
                    return i
                b.step(f"y{c}", go)

            def y_deltas():
                b.wait(pool, "y_prod3")
                y = y_ps[prv.par][:, :].rearrange("p (j n) -> p j n", j=C)

                def go():
                    at = 0
                    for d in range(C):
                        i = mm(y[:, d:C, :], ident[:, :], y_prod[:, at:at + C - d, :], start=False, stop=True,
                               skip_group_check=True)
                        at += C - d
                    return i
                b.step("y", go)

            def y_mean():
                b.wait(act, "y_sq")
                b.wait(act, "x1_ct", back=1)
                b.step("ms", lambda: mm(post_ps[0][:, :], heads_mean[:, :], y_sq[:, :], start=True, stop=True))

            def out_proj():
                if not b.dry:
                    b.dma(s_xtc, prv)
                b.wait(dve, "logits", back=1)
                b.step("res", lambda: mm(post_ps[1][:, :], ident[:, :], x_tc[:, :], start=True, stop=False,
                                         skip_group_check=True))
                b.wait(pool, "ctx")

                def go():
                    mm(post_ps[1][:, :], ones[0:1, :], bias_o[0:1, :], start=False, stop=False, skip_group_check=True)
                    for i in range(TW):
                        last = mm(post_ps[1][:, i * D:(i + 1) * D], ctx_t[:, i * P:(i + 1) * P], w_o[:, :],
                                  start=False, stop=True, skip_group_check=True)
                    return last
                b.step("attn", go)

            def turn():
                b.wait(dve, f"x1_{TW - 1}")
                b.wait(act, "rms")

                def go():
                    for i in range(TW):
                        last = tr(post_ps[0][:, i * P:(i + 1) * P], x1[:, i, :], ident[:, :])
                    return last
                b.step("turn", go)

            def router():
                b.wait(act, "x1_ct")
                b.wait(dve, f"x1_{TW - 1}")

                def go():
                    for i in range(TW):
                        last = mm(post_ps[1][:, i * E:(i + 1) * E], x1_ct[:, i, :], w_r[:, :], start=True, stop=True)
                    return last
                b.step("router", go)

            if post:
                y_deltas()
            if pre:
                if not b.dry:
                    b.dma(s_xct, nxt)
                project("z", 5, 0, (dve, "aqk_far"), 1)
                project("b", 4, 1, (dve, "akk_far"), 1)
                project("k", 1, 2, (act, "aqk_same"), 1)
                project("q", 0, 3, (dve, "aqk_near"), 1)
                project("v", 2, 0, (act, "z_abs"))
                project("g", 3, 1, (act, "b_abs"))
            if post:
                y_mean()
            if chain:
                y_chunk(0)
            if pre:
                head_sum("nk", k_sq[:, :], 2, (act, "k_sq"), (act, "k_s"))
                head_sum("nq", q_sq[:, :], 3, (act, "q_sq"), (act, "q_s"))
            if chain:
                y_chunk(1)
            if post:
                out_proj()
            if chain:
                y_chunk(2)
                y_chunk(3)
            if pre:
                kkf, qkf = (x[:, :, :].rearrange("p s n -> p (s n)") for x in (kk, qk))
                head_sum("kk_near", kkf[:, 0:3 * NN], 0, (pool, "kk_near"), (dve, "beta_v"))
                head_sum("kk_far", kkf[:, 3 * NN:6 * NN], 1, (pool, "kk_far2"), (act, "g_abs"))
            if post:
                turn()
            if chain:
                y_chunk(4)
            if pre:
                head_sum("qk_same", qkf[:, 0:4 * NN], 2, (pool, "qk_same"), (act, "nk_ln"))
                head_sum("qk_near", qkf[:, 4 * NN:7 * NN], 3, (pool, "qk_near"), (act, "nq_ln"))
            if post:
                router()
            if chain:
                y_chunk(5)
            if pre:
                head_sum("qk_far", qkf[:, 7 * NN:10 * NN], 0, (pool, "qk_far2"), (dve, "akk_near"))
            if chain:
                y_chunk(6)
                y_chunk(7)

        def act_body(b):
            w = b.win
            pre, post = HAS_PRE[b.kind], HAS_POST[b.kind]
            nxt, prv = w.shift(1), w.shift(-1)
            A = nc.scalar.activation

            def soft(name, bank, src_label, r, a, sign, bias=None):
                extra = {} if bias is None else {"bias": bias}
                b.wait(pe, src_label)
                b.step(f"{name}_relu", lambda: A(r[:, :], ring[bank][:, :], ACT.Relu, scale=sign, **extra))
                b.step(f"{name}_abs", lambda: A(a[:, :], ring[bank][:, :], ACT.Abs, scale=sign, **extra))
                b.own()
                b.step(f"{name}_exp", lambda: A(a[:, :], a[:, :], ACT.Exp, scale=-1.0))
                b.own()
                b.step(f"{name}_ln", lambda: A(a[:, :], a[:, :], ACT.Ln, bias=1.0))

            if pre:
                b.wait(pool, "pre_end", back=1)
                b.wait(dve, "aqk_far", back=1)
                b.wait(pe, "qk_far", back=1)
                b.wait(act, "to_end0", back=1)
                if not b.dry and not (isinstance(w.w, int) and w.w < 0):
                    b.dma1(s_kout, w)
                    b.dma1(s_qout, w)
                soft("z", 0, "z", z_r, z_a, 1.0, dt_b[:, 0:1])
                soft("b", 1, "b", b_r, b_a, -1.0)
            if post:
                b.wait(pe, "y")
                b.wait(dve, "y_n", back=1)
                b.wait(pe, "router", back=1)
                b.step("y_sq", lambda: A(y_sq[:, :], y_ps[prv.par][:, :], ACT.Square))
            if pre:
                for n, bank, s, sq in (("k", 2, k_s, k_sq), ("q", 3, q_s, q_sq)):
                    b.wait(pe, n)
                    b.step(f"{n}_sq", lambda: A(sq[:, :], ring[bank][:, :], ACT.Square))
                    b.step(f"{n}_s", lambda: A(s[:, :], ring[bank][:, :], ACT.Copy))
                b.wait(pool, "z_sum")
                b.step("alpha", lambda: A(alpha[:, :], z_a[:, :], ACT.Exp, scale=neg_a[:, 0:1]))
                b.wait(pool, "b_sum")
                b.step("beta", lambda: A(beta[:, :], b_a[:, :], ACT.Exp, scale=-1.0))
            if post:
                b.wait(pe, "ms")
                b.step("rms", lambda: A(y_sq[:, :], post_ps[0][:, :], ACT.Ln, bias=rms_eps[:, 0:1]))
                b.own()
                b.step("rms_r", lambda: A(y_sq[:, :], y_sq[:, :], ACT.Exp, scale=-0.5))
            if pre:
                for n, bank, sq, bias in (("nk", 2, k_sq, None), ("nq", 3, q_sq, q_bias[:, 0:1])):
                    extra = {} if bias is None else {"bias": bias}
                    b.wait(pe, n)
                    b.step(f"{n}_ln", lambda: A(sq[:, :], ring[bank][:, :], ACT.Ln))
                    b.own()
                    b.step(f"{n}_r", lambda: A(sq[:, :], sq[:, :], ACT.Exp, scale=-0.5, **extra))
                b.wait(pe, "g")
                b.wait(pool, "ctx")
                b.wait(pool, "z_sum")
                b.wait(act, "beta")
                b.step("g_s", lambda: A(gate[nxt.par][:, :], ring[1][:, :], ACT.Copy, scale=norm_w[:, 0:1]))
                soft("g", 1, "g", g_r, g_a, -1.0)
            if post:
                b.wait(dve, f"mv{TW - 1}")
                b.wait(dve, f"x1_{TW - 1}", back=1)
                b.step("ln_ln", lambda: A(rstd[:, :], mv[:, :, 1], ACT.Ln, bias=ln_eps[:, 0:1]))
                b.own()
                b.step("ln_r", lambda: A(rstd[:, :], rstd[:, :], ACT.Exp, scale=-0.5))
                b.wait(dve, f"x1_{TW - 1}")
                at = prv.w * TW
                b.step("x1_keep", lambda: A(x1_all[:, bass.ds(at, TW), :], x1[:, :, :], ACT.Copy))
                b.wait(pe, "turn")
                b.wait(dve, "y_n")
                b.step("x1_ct", lambda: A(x1_ct, post_ps[0][:, :].rearrange("p (i n) -> p i n", i=TW), ACT.Copy))
            if pre:
                b.wait(pool, "g_sum")
                b.step("g_sig", lambda: A(g_r[:, :], g_a[:, :], ACT.Exp, scale=-1.0))
                b.wait(dve, "d_end7", back=1)
                b.wait(pool, "far2")
                b.step("to_end2", lambda: A(to_end[nxt.par][:, 2, :], slots(alpha)[:, 3, :], ACT.Copy))
                b.step("to_end1", lambda: A(to_end[nxt.par][:, 1, :], far[:, 1, :], ACT.Copy))
                b.wait(pe, "qk_same")
                b.wait(pool, "y_prod3")
                b.step("aqk_same", lambda: A(aqk[nxt.par][:, 0:4, :].rearrange("p s n -> p (s n)"), ring[2][:, :], ACT.Copy))
                b.step("to_end0", lambda: A(to_end[nxt.par][:, 0, :], far[:, 2, :], ACT.Copy))

        def pool_body(b):
            w = b.win
            pre, chain, post = HAS_PRE[b.kind], HAS_CHAIN[b.kind], HAS_POST[b.kind]
            nxt, prv = w.shift(1), w.shift(-1)
            tt = nc.gpsimd.tensor_tensor

            def mul(label, out, x, y, op=ALU.mult):
                b.step(label, lambda: tt(out, x, y, op))

            def q_times_s(c):
                if c == 0:
                    if not b.dry:
                        b.dma(s_qrep, w)
                    b.wait(dve, "S7", back=1)
                    b.wait(pe, "y6", back=1)
                else:
                    b.wait(dve, f"S{c - 1}")
                if c == 1:
                    b.wait(pe, "y7", back=1)
                if c >= 2:
                    b.wait(pe, f"y{c - 2}")
                s = S[c % 2][:, :, :].rearrange("p b d -> p d b").unsqueeze(2).to_broadcast([P, DH, C, NB])
                mul(f"q_prod{c}", q_prod[c % 2][:, :, :, :], s, rep_chunk(q_rep[w.par], c, "d j b"))

            if chain:
                q_times_s(0)
            if post:
                b.wait(dve, "d_end7", back=1)
                b.wait(pe, "qk_far", back=1)
                dl, aq, at = delta[prv.par], aqk[prv.par], 0
                for d in range(C):
                    mul(f"y_prod{d}", y_prod[:, at:at + C - d, :], aq[:, at:at + C - d, :], dl[:, 0:C - d, :])
                    at += C - d
            if pre:
                b.wait(act, "z_ln")
                mul("z_sum", z_a[:, :], z_a[:, :], z_r[:, :], ALU.add)
                b.wait(act, "b_ln")
                mul("b_sum", b_a[:, :], b_a[:, :], b_r[:, :], ALU.add)
            if chain:
                q_times_s(1)
            if pre:
                al, bt = slots(alpha), slots(beta)
                gm = slots(gam[nxt.par])
                b.wait(act, "alpha")
                b.wait(dve, "upd7", back=1)
                mul("far0", far[:, 0:2, :], al[:, 2:4, :], al[:, 1:3, :])
                b.step("gam0", lambda: nc.gpsimd.tensor_copy(gm[:, 0, :], al[:, 0, :]))
                mul("gam1", gm[:, 1, :], al[:, 0, :], al[:, 1, :])
                b.own()
                mul("far2", far[:, 2, :], far[:, 1, :], al[:, 1, :])
                mul("gam2", gm[:, 2, :], gm[:, 1, :], al[:, 2, :])
                b.own()
                mul("gam3", gm[:, 3, :], gm[:, 2, :], al[:, 3, :])
                b.wait(act, "beta")
                mul("beta_near", beta_near[:, :, :], bt[:, 1:4, :], al[:, 1:4, :])
                mul("beta_far", beta_far[:, 0:2, :], bt[:, 2:4, :], far[:, 0:2, :])
                mul("beta_far2", beta_far[:, 2, :], bt[:, 3, :], far[:, 2, :])
                b.wait(pool, "gam3")
                mul("beta_gam", beta_gam[nxt.par][:, :], beta[:, :], gam[nxt.par][:, :])
            if chain:
                q_times_s(2)
            if pre:
                b.wait(act, "nk_r")
                mul("k_n", k_s[:, :], k_s[:, :], k_sq[:, :])
                b.wait(act, "nq_r")
                mul("q_n", q_s[:, :], q_s[:, :], q_sq[:, :])
                b.own()
                mul("q_gam", q_sq[:, :], q_s[:, :], gam[nxt.par][:, :])
            if post:
                b.wait(dve, "y_n")
                b.wait(pe, "attn", back=1)
                mul("ctx", slots(ctx_t), y_n.rearrange("p (j n) -> p j n", j=C), slots(gate[prv.par]))
            if chain:
                q_times_s(3)
            if pre:
                kn, qn = slots(k_s), slots(q_s)
                mul("kk_near", kk[:, 0:3, :], kn[:, 1:4, :], kn[:, 0:3, :])
                mul("kk_far", kk[:, 3:5, :], kn[:, 2:4, :], kn[:, 0:2, :])
                mul("kk_far2", kk[:, 5, :], kn[:, 3, :], kn[:, 0, :])
                b.wait(act, "g_ln")
                mul("g_sum", g_a[:, :], g_a[:, :], g_r[:, :], ALU.add)
            if chain:
                q_times_s(4)
            if pre:
                b.wait(pe, "y")
                mul("qk_same", qk[:, 0:4, :], qn, kn)
                mul("qk_near", qk[:, 4:7, :], qn[:, 1:4, :], kn[:, 0:3, :])
                mul("qk_far", qk[:, 7:9, :], qn[:, 2:4, :], kn[:, 0:2, :])
                mul("qk_far2", qk[:, 9, :], qn[:, 3, :], kn[:, 0, :])
            if chain:
                q_times_s(5)
                q_times_s(6)
            if pre:
                b.wait(act, "g_sig")
                b.wait(pool, "ctx")
                mul("pre_end", gate[nxt.par][:, :], gate[nxt.par][:, :], g_r[:, :])
            if chain:
                q_times_s(7)

        def dve_body(b):
            w = b.win
            pre, chain, post = HAS_PRE[b.kind], HAS_CHAIN[b.kind], HAS_POST[b.kind]
            nxt, prv = w.shift(1), w.shift(-1)
            v = nc.vector

            chained = []

            def link(label, ins):
                if chained:
                    b.wait(dve, chained[-1])
                b.step(label, ins)
                chained.append(label)

            def chunk(c):
                kr, dl = k_rep[w.par], slot_chunk(delta[w.par], c)
                s_in, s_out = S[c % 2], S[(c + 1) % 2]
                if c == 0:
                    if not b.dry:
                        b.dma(s_krep, w)
                    b.wait(pool, "beta_gam", back=1)
                    b.wait(act, "to_end0", back=1)
                    b.wait(pool, "y_prod3", back=1)
                    b.wait(dve, "S7", back=1)
                    b.wait(dve, "akk_far", back=1)
                    b.wait(dve, "beta_v", back=1)
                link(f"k_prod{c}", lambda: v.tensor_tensor(
                    prod, s_in[:, :, :].unsqueeze(1).to_broadcast([P, C, NB, DH]),
                    rep_chunk(kr, c, "j b d"), ALU.mult))
                link(f"k_sum{c}", lambda: v.tensor_reduce(
                    ks[:, :, :].rearrange("p j b -> p (j b)"), prod.rearrange("p j b d -> p (j b) d"),
                    AX, ALU.add))
                link(f"k_gam{c}", lambda: v.tensor_tensor(ks[:, :, :], ks[:, :, :], chunk_jb(beta_gam[w.par], c), ALU.mult))
                link(f"rhs{c}", lambda: v.tensor_tensor(dl, chunk_jb(beta_v[w.par], c), ks[:, :, :], ALU.subtract))
                for s in range(C - 1):
                    n = C - 1 - s
                    a = slot_chunk(akk[w.par], c)[:, s:s + C * (n - 1) + 1:C, :]
                    link(f"tri{s}_{c}", lambda: v.tensor_tensor(
                        tri[:, 0:n, :], a, dl[:, s:s + 1, :].to_broadcast([P, n, NB]), ALU.mult))
                    link(f"sub{s}_{c}", lambda: v.tensor_tensor(dl[:, s + 1:C, :], dl[:, s + 1:C, :], tri[:, 0:n, :], ALU.subtract))
                b.step(f"decay{c}", lambda: v.tensor_tensor(
                    upd[:, :, :, C], s_in[:, :, :],
                    chunk_jb(gam[w.par], c)[:, C - 1, :].unsqueeze(2).to_broadcast([P, NB, DH]), ALU.mult))
                link(f"d_end{c}", lambda: v.tensor_tensor(d_end[:, :, :], dl, slot_chunk(to_end[w.par], c), ALU.mult))
                link(f"upd{c}", lambda: v.tensor_tensor(
                    upd[:, :, :, 0:C], rep_chunk(kr, c, "b d j"),
                    d_end[:, :, :].rearrange("p j b -> p b j").unsqueeze(2).to_broadcast([P, NB, DH, C]), ALU.mult))
                if c:
                    b.wait(pool, f"q_prod{c - 1}")
                else:
                    b.wait(pool, "q_prod7", back=1)
                link(f"S{c}", lambda: v.tensor_reduce(
                    s_out[:, :, :].rearrange("p b d -> p (b d)"), upd[:, :, :, :].rearrange("p b d s -> p (b d) s"),
                    AX, ALU.add))

            if chain:
                chunk(0)
                chunk(1)
            if pre:
                b.wait(act, "beta")
                b.wait(pe, "v")
                b.wait(dve, "rhs7", back=1)
                b.step("beta_v", lambda: v.tensor_tensor(beta_v[nxt.par][:, :], ring[0][:, :], beta[:, :], ALU.mult))
            if post:
                b.wait(act, "rms_r")
                b.wait(pe, "y")
                b.wait(act, "x1_keep", back=1)
                b.wait(pe, "turn", back=1)
                b.step("y_n", lambda: v.tensor_tensor(y_n, y_ps[prv.par][:, :], y_sq[:, :], ALU.mult))
            if chain:
                chunk(2)
                chunk(3)
            if post:
                b.wait(pe, "attn")
                b.wait(dve, f"x1_{TW - 1}", back=1)
                for i in range(TW):
                    b.step(f"stats{i}", lambda: v.bn_stats(stats[:, i, :], post_ps[1][:, i * D:(i + 1) * D]))
            if chain:
                chunk(4)
            if post:
                if not chain:
                    b.own()
                for i in range(TW):
                    b.step(f"mv{i}", lambda: v.bn_aggr(mv[:, i, :], stats[:, i, :]))
            if chain:
                chunk(5)
            if post:
                b.wait(act, "ln_r")
                b.wait(pool, "ctx")
                for i in range(TW):
                    b.step(f"x1_{i}", lambda: v.tensor_scalar(x1[:, i, :], post_ps[1][:, i * D:(i + 1) * D], mv[:, i, 0:1],
                                                              rstd[:, i:i + 1], ALU.subtract, ALU.mult))
            if pre:
                ak, aq = akk[nxt.par], aqk[nxt.par]

                def r3(bank):
                    return ring[bank][:, 0:3 * NN].rearrange("p (s n) -> p s n", s=3)
                b.wait(pe, "kk_near")
                b.wait(pool, "beta_far2")
                b.step("akk_near", lambda: v.tensor_tensor(ak[:, 0:3, :], r3(0), beta_near[:, :, :], ALU.mult))
                b.wait(pe, "kk_far")
                b.step("akk_far2", lambda: v.tensor_tensor(ak[:, 8, :], r3(1)[:, 2, :], beta_far[:, 2, :], ALU.mult))
                b.step("akk_far", lambda: v.tensor_tensor(ak[:, 4:6, :], r3(1)[:, 0:2, :], beta_far[:, 0:2, :], ALU.mult))
            if chain:
                chunk(6)
            if post:
                b.wait(pe, "router")
                at = prv.w * TW
                b.step("logits", lambda: v.tensor_copy(logits[:, bass.ds(at, TW), :],
                                                       post_ps[1][:, 0:TW * E].rearrange("p (i e) -> p i e", i=TW)))
            if pre:
                b.wait(pe, "qk_near")
                b.wait(pool, "y_prod3")
                b.step("aqk_near", lambda: v.tensor_tensor(aq[:, 4:7, :], r3(3), slots(alpha)[:, 1:4, :], ALU.mult))
                b.wait(pe, "qk_far")
                b.step("aqk_far", lambda: v.tensor_tensor(aq[:, 7:10, :], r3(0), far[:, :, :], ALU.mult))
            if chain:
                chunk(7)

        def sp_body(b):
            w = b.win
            pre, chain, post = HAS_PRE[b.kind], HAS_CHAIN[b.kind], HAS_POST[b.kind]
            nxt, prv, far2 = w.shift(1), w.shift(-1), w.shift(2)
            e = b.eng
            if chain:
                if not (isinstance(w.w, int) and w.w + 2 >= NW):
                    b.wait(pe, "g", back=1)
                    e.dma_start(x_ct[w.par][:, :], t["x_ct"][:, bass.ds(far2.w, 1), :].rearrange("p o n -> p (o n)")) \
                        .then_inc(s_xct[w.par], 16)
            if pre:
                if not (isinstance(w.w, int) and w.w <= 0):
                    b.dma(s_krep, prv)
                    b.dma(s_qrep, prv)
                b.wait(pool, "k_n")
                e.dma_start(t["k_dram"][nxt.par], k_s[:, :]).then_inc(s_kout, 16)
                b.wait(pool, "q_gam")
                e.dma_start(t["q_dram"][nxt.par], q_sq[:, :]).then_inc(s_qout, 16)
                for name, dst, s_out, s_rep in (("k_dram", k_rep, s_kout, s_krep), ("q_dram", q_rep, s_qout, s_qrep)):
                    b.dma1(s_out, nxt)
                    src = t[name][nxt.par].rearrange("(h d) n -> h (d n)", d=DH).unsqueeze(1).to_broadcast([H, DH, DH * WN])
                    e.dma_start(dst[nxt.par][:, :, :].rearrange("p d n -> p (d n)"), src).then_inc(s_rep[nxt.par], 16)
            if chain:
                b.wait(pe, "res")
                e.dma_start(x_tc[:, :], t["x_tc"][bass.ds(w.w, 1), :, :].rearrange("o p n -> (o p) n")) \
                    .then_inc(s_xtc[w.par], 16)

        def windows(steps, eng, body, setup):
            def run(kind, win):
                body(Body(steps, eng, kind, win, False))
            setup(eng)
            run(PRE_ONLY, Win(-1, 1))
            run(FIRST, Win(0, 0))
            run(FULL, Win(0, 1))
            with eng.Fori(1, NW // 2 - 1) as i:
                run(FULL, Win(i, 0))
                run(FULL, Win(i, 1))
            run(FULL, Win(NW // 2 - 1, 0))
            run(LAST, Win(NW // 2 - 1, 1))
            run(POST_ONLY, Win(NW // 2, 0))

        for steps, body in ((pe, pe_body), (act, act_body), (pool, pool_body), (dve, dve_body)):
            for kind in range(5):
                body(Body(steps, None, kind, Win(0, 0), True))

        n_const = 16 * (len(t["consts"]) + 4)
        n_setup = 9
        tiles = dict(w_q=w_proj[:, 0, :], w_k=w_proj[:, 1, :], w_v=w_proj[:, 2, :], w_g=w_proj[:, 3, :],
                     w_b=w_proj[:, 4, :], w_a=w_a[:, :], w_o=w_o[:, :], w_r=w_r[:, :], ident=ident[:, :],
                     heads=heads[:, :], heads_mean=heads_mean[:, :], below=below[:, :], ones=ones[:, :],
                     iota_e=iota_e[:, :], iota_t=iota_t[:, :])

        @block.sync
        def _(eng):
            def setup(e):
                for name, src in t["consts"].items():
                    e.dma_start(tiles[name], src).then_inc(s_const, 16)
                for n in range(2):
                    e.dma_start(x_ct[n][:, :], t["x_ct"][:, n, :]).then_inc(s_xct[n], 16)
                e.dma_start(dt_b[:, :], t["dt_bias"].rearrange("(h o) -> h o", o=1).unsqueeze(1).to_broadcast([H, DH, 1])).then_inc(s_const, 16)
                e.dma_start(neg_a[:, :], t["A_log"].rearrange("(h o) -> h o", o=1).unsqueeze(1).to_broadcast([H, DH, 1])).then_inc(s_const, 16)
                e.dma_start(norm_w[:, :], t["norm_w"].rearrange("(d o) -> d o", o=1).unsqueeze(0).to_broadcast([H, DH, 1])).then_inc(s_const, 16)
                e.dma_start(bias_o[:, :].rearrange("o (i n) -> o i n", n=D), t["bo"].rearrange("(o n) -> o n", o=1).unsqueeze(1).to_broadcast([1, TW, D])).then_inc(s_const, 16)
                e.wait_ge(s_setup, n_setup)
                e.dma_start(t["x_sorted"].rearrange("(m p) d -> p m d", p=P),
                            zero[:, :].unsqueeze(1).to_broadcast([P, MT, D])).then_inc(s_pad, 16)
            windows(Steps(None), eng, sp_body, setup)
            finish_sync(eng)


        @block.tensor
        def _(eng):
            def setup(e):
                e.wait_ge(s_const, n_const)
                e.wait_ge(s_setup, n_setup)
            windows(pe, eng, pe_body, setup)
            finish_pe(eng)

        @block.scalar
        def _(eng):
            def setup(e):
                e.wait_ge(s_const, n_const)
                e.wait_ge(s_setup, n_setup)
                nc.scalar.activation(neg_a[:, :], neg_a[:, :], ACT.Exp).then_inc(s_zero, 1)
                e.wait_ge(s_zero, 1)
                nc.scalar.mul(neg_a[:, :], neg_a[:, :], -1.0).then_inc(s_zero, 1)
                e.wait_ge(s_zero, 2)
            windows(act, eng, act_body, setup)
            finish_act(eng)

        @block.gpsimd
        def _(eng):
            def setup(e):
                e.wait_ge(s_setup, n_setup)
            windows(pool, eng, pool_body, setup)
            finish_pool(eng)

        @block.vector
        def _(eng):
            def setup(e):
                import math
                for n in range(2):
                    nc.vector.memset(S[n][:, :, :], 0.0).then_inc(s_setup, 1)
                    nc.vector.memset(to_end[n][:, C - 1, :], 1.0).then_inc(s_setup, 1)
                nc.vector.memset(zero[:, :], 0.0).then_inc(s_setup, 1)
                nc.vector.memset(q_bias[:, :], -0.5 * math.log(DH)).then_inc(s_setup, 1)
                nc.vector.memset(rms_eps[:, :], RMS_EPS).then_inc(s_setup, 1)
                e.wait_ge(s_const, n_const)
                nc.vector.memset(ln_eps[:, :], LN_EPS).then_inc(s_setup, 1)
                nc.vector.tensor_copy(w_proj[:, 5, :].rearrange("p (h d) -> p h d", d=DH),
                                      w_a[:, :].unsqueeze(2).to_broadcast([P, H, DH])).then_inc(s_setup, 1)
                e.wait_ge(s_setup, n_setup)
            windows(dve, eng, dve_body, setup)
            finish_dve(eng)


def kernel(**inputs):
    import numpy as _np
    import concourse.bacc as _bacc
    from concourse import mybir as _mybir
    from concourse.bass_utils import run_bass_kernel_spmd as _run

    a = {k: _np.ascontiguousarray(v) for k, v in inputs.items()}
    f = _np.float32
    x = a["L0_attn_x"]
    chan = _np.arange(P)
    same_head = (chan[:, None] // DH == chan[None, :] // DH).astype(f)
    down = _np.zeros((E, IC * P, D), a["L0_ffn_down_w"].dtype)
    down[:, :I, :] = a["L0_ffn_down_w"].transpose(0, 2, 1)
    arrays = {
        "x_ct": x.reshape(NB, NW, T, D).transpose(3, 1, 0, 2).reshape(D, NW, WN),
        "x_tc": x.reshape(TW, NB // TW, NW, T, D).transpose(2, 1, 3, 0, 4).reshape(NW, P, TW * D),
        "w_q": a["L0_attn_Wq"].T, "w_k": a["L0_attn_Wk"].T, "w_v": a["L0_attn_Wv"].T,
        "w_g": a["L0_attn_Wg"].T, "w_b": a["L0_attn_Wb"].T, "w_a": a["L0_attn_Wa"].T,
        "w_o": a["L0_attn_Wo"].T, "w_r": a["L0_ffn_router_w"].T,
        "dt_bias": a["L0_attn_dt_bias"], "A_log": a["L0_attn_A_log"], "norm_w": a["L0_attn_norm_w"],
        "bo": a["L0_attn_bo"],
        "gate_w": a["L0_ffn_gate_w"].transpose(2, 0, 1), "up_w": a["L0_ffn_up_w"].transpose(2, 0, 1),
        "down_w": down.reshape(E, IC, P, D).transpose(2, 1, 0, 3),
        "ident": _np.eye(P, dtype=f), "heads": same_head, "heads_mean": same_head / f(DH),
        "below": (chan[:, None] < chan[None, :]).astype(f), "ones": _np.ones((P, P), f),
        "iota_e": _np.tile(_np.arange(E, dtype=f), (P, 1)), "iota_t": _np.arange(MT, dtype=f)[None, :],
    }
    arrays = {k: _np.ascontiguousarray(v) for k, v in arrays.items()}
    nc = _bacc.Bacc("TRN2", target_bir_lowering=False, num_devices=1)
    dram = {k: nc.dram_tensor(f"in_{k}", v.shape, _mybir.dt.from_np(v.dtype), kind="ExternalInput").ap()
            for k, v in arrays.items()}
    names = ("w_q", "w_k", "w_v", "w_g", "w_b", "w_a", "w_o", "w_r", "ident", "heads", "heads_mean", "below", "ones",
             "iota_e", "iota_t")
    dram["consts"] = {k: dram[k] for k in names}
    dram["k_dram"] = [nc.dram_tensor(f"k_dram{n}", (P, WN), F32, kind="Internal").ap() for n in range(2)]
    dram["q_dram"] = [nc.dram_tensor(f"q_dram{n}", (P, WN), F32, kind="Internal").ap() for n in range(2)]
    dram["x_sorted"] = nc.dram_tensor("x_sorted", (MT * P, D), F32, kind="Internal").ap()
    dram["y_sorted"] = nc.dram_tensor("y_sorted", (MT * P, D), F32, kind="Internal").ap()
    dram["out"] = nc.dram_tensor("out_0", (NW, P, TW * D), F32, kind="ExternalOutput").ap()
    block_kernel(nc, dram)
    r = _run(nc, [{f"in_{k}": v for k, v in arrays.items()}], core_ids=[0])
    y = r.results[0]["out_0"].reshape(NW, NB // TW, T, TW, D)
    return _np.ascontiguousarray(y.transpose(3, 1, 0, 2, 4).reshape(NB, L, D))
```

```python
from contextlib import ExitStack

import concourse.bass as bass
from concourse import mybir

F32 = mybir.dt.float32
I32 = mybir.dt.int32
ALU = mybir.AluOpType
ACT = mybir.ActivationFunctionType
AX = mybir.AxisListType.X

P = 128
NB, L, D = 16, 512, 128
H, DH = 16, 8
T, C = 32, 4
NW, NCH = L // T, T // C
WN = NB * T
NN = NB * NCH
TW = WN // P
NT = NW * TW
E, I = 8, 352
IC = (I + P - 1) // P
MT = NT + E
NS = 4
LN_EPS, RMS_EPS = 1e-5, 1e-6

PRE_ONLY, FIRST, FULL, LAST, POST_ONLY = range(5)
HAS_PRE = (True, True, True, False, False)
HAS_CHAIN = (False, True, True, True, False)
HAS_POST = (False, False, True, True, True)


class Win:

    def __init__(self, i, par):
        self.i, self.par = i, par

    @property
    def w(self):
        return self.i * 2 + self.par

    def shift(self, n):
        return Win(self.i + (self.par + n) // 2, (self.par + n) % 2)


class Steps:

    def __init__(self, sem):
        self.sem, self.order, self.kind = sem, {}, None

    def count(self, kind):
        return len(self.order[kind])

    def value(self, label, kind, body):
        at = self.order[kind].index(label) + 1
        if kind == PRE_ONLY:
            return at
        at = at + self.count(PRE_ONLY)
        if kind == FIRST:
            return at
        at = at + self.count(FIRST)
        if kind == POST_ONLY:
            return at + (NW - 2) * self.count(FULL) + self.count(LAST)
        return (body - 1) * self.count(FULL) + at


def kind_of(win, first, last):
    return FIRST if first else LAST if last else FULL


def block_kernel(nc, t):
    ctx = ExitStack()
    with ctx:
        def sb(name, shape, dt=F32):
            return ctx.enter_context(nc.sbuf_tensor(name, shape, dt))

        def sem(name):
            return ctx.enter_context(nc.semaphore(name))

        def two(name, shape):
            return [sb(f"{name}{n}", shape) for n in range(2)]

        w_proj = sb("w_proj", [P, 6, D])
        w_a = sb("w_a", [P, H])
        w_o = sb("w_o", [P, D])
        w_r = sb("w_r", [P, E])
        ident = sb("ident", [P, P])
        heads = sb("heads", [P, P])
        heads_q = sb("heads_q", [P, P])
        heads_mean = sb("heads_mean", [P, P])
        below = sb("below", [P, P])
        ones = sb("ones", [P, P])
        bias_o = sb("bias_o", [1, D])
        iota_e = sb("iota_e", [P, E])
        iota_t = sb("iota_t", [1, MT])
        neg_a = sb("neg_a", [P, 1])
        norm_w = sb("norm_w", [P, 1])
        dt_row = sb("dt_row", [1, P])
        dt_in = sb("dt_in", [1, H])
        rms_eps = sb("rms_eps", [P, 1])
        ln_eps = sb("ln_eps", [P, 1])
        zero = sb("zero", [P, D])
        x1_all = sb("x1_all", [P, NT, D])
        logits = sb("logits", [P, NT, E])
        stats = sb("stats", [P, TW, 6])
        mv = sb("mv", [P, TW, 2])
        rstd = sb("rstd", [P, TW])
        shift = sb("shift", [P, TW])
        settle = sb("settle", [P, 1])

        att = ExitStack()
        att.__enter__()

        def sa(name, shape):
            return att.enter_context(nc.sbuf_tensor(name, shape, F32))

        def two_a(name, shape):
            return [sa(f"{name}{n}", shape) for n in range(2)]

        x_ct = two_a("x_ct", [P, WN])
        x_tc = sa("x_tc", [P, TW * D])
        k_rep = two_a("k_rep", [P, DH, WN])
        q_rep = two_a("q_rep", [P, DH, WN])
        beta_v = two_a("beta_v", [P, WN])
        beta_gam = two_a("beta_gam", [P, WN])
        gam = two_a("gam", [P, WN])
        to_end = two_a("to_end", [P, C, NN])
        akk = two_a("akk", [P, 9, NN])
        aqk = two_a("aqk", [P, 10, NN])
        delta = two_a("delta", [P, C, NN])
        gate_in = sa("gate_in", [P, WN])
        gate = two_a("gate", [P, WN])
        zbg_r = sa("zbg_r", [P, 3, WN])
        zbg_a = sa("zbg_a", [P, 3, WN])
        alpha, beta, g_sig = (zbg_a[:, n, :] for n in range(3))
        spare = zbg_r[:, :, :].rearrange("p a (b n) -> p (a b) n", n=NN)
        kk, beta_near, beta_far = spare[:, 0:6, :], spare[:, 6:9, :], spare[:, 9:12, :]
        kq_s, kq_sq = sa("kq_s", [P, 2, WN]), sa("kq_sq", [P, 2, WN])
        k_s, q_s, q_scaled = kq_s[:, 0, :], kq_s[:, 1, :], kq_sq[:, 1, :]
        far = sa("far", [P, 3, NN])
        qk = sa("qk", [P, 10, NN])
        S = [sa(f"S{n}", [P, NB, DH]) for n in range(NS)]
        ks = sa("ks", [P, C, NB])
        tri = sa("tri", [P, C - 1, NB])
        d_end = sa("d_end", [P, C, NB])
        upd = sa("upd", [P, NB, DH, C + 1])
        q_prod = [sa(f"q_prod{n}", [P, DH, 2, C, NB]) for n in range(3)]
        q_prod = [q_prod[n] for n in (0, 1, 2, 1)]
        y_prod = qk
        y_sq = sa("y_sq", [P, WN])
        ctx_t = sa("ctx_t", [P, WN])
        x1 = sa("x1", [P, TW, D])
        y_n = x1[:, :, :].rearrange("p i n -> p (i n)")
        x1_ct = y_sq[:, :].rearrange("p (i n) -> p i n", i=TW)

        psum = ctx.enter_context(nc.psum_tensor("banks", [P, 8, WN], F32))
        pb = [psum[:, n, :] for n in range(8)]
        zbg_ps, kq_ps = psum[:, 0:3, :], psum[:, 3:5, :]
        y_ps, post_ps = pb[5:7], pb[7]

        s_const = sem("s_const")
        s_setup = sem("s_setup")
        s_zero = sem("s_zero")
        s_xct = [sem(f"s_xct{n}") for n in range(2)]
        s_xtc = [sem(f"s_xtc{n}") for n in range(2)]
        s_kout, s_qout = sem("s_kout"), sem("s_qout")
        s_krep, s_qrep = ([sem(f"s_{n}rep{m}") for m in range(2)] for n in "kq")
        act, dve, pool, pe = (Steps(sem(f"s_{n}")) for n in ("act", "dve", "pool", "pe"))

        att.close()
        U = 4
        gate_we = sb("gate_we", [P, E, I])
        up_we = sb("up_we", [P, E, I])
        down_we = sb("down_we", [P, IC, E, D])
        top = sb("top", [P, NT])
        cand = sb("cand", [P, NT, E])
        one_hot = sb("one_hot", [P, NT, E])
        total = sb("total", [P, NT, E])
        before = sb("before", [P, NT, E])
        tiles_i = sb("tiles_i", [P, E], I32)
        tiles_f = sb("tiles_f", [P, E])
        tile_end = sb("tile_end", [P, E])
        place_f = sb("place_f", [P, NT])
        place = sb("place", [P, NT], I32)
        past = sb("past", [1, MT, E])
        expert_f = sb("expert_f", [1, MT])
        expert_at = sb("expert_at", [1, MT], I32)
        xs = [sb(f"xs{n}", [P, D]) for n in range(U)]
        ys = [sb(f"ys{n}", [P, D]) for n in range(U)]
        xs_t = two("xs_t", [P, P])
        silu = two("silu", [P, I])
        hid = two("hid", [P, IC * P])
        hid_t = two("hid_t", [P, IC, P])
        back_y = two("back_y", [P, TW, D])
        res_y = two("res_y", [P, TW, D])
        out_y = two("out_y", [P, TW, D])

        s_wexp = sem("s_wexp")
        s_route, s_count, s_pad = sem("s_route"), sem("s_count"), sem("s_pad")
        s_sorted, s_back = sem("s_sorted"), [sem(f"s_back{n}") for n in range(2)]
        s_xs, s_ys = ([sem(f"s_{m}{n}") for n in range(U)] for m in ("xs", "ys"))
        s_xturn, s_xt, s_up, s_silu, s_hid, s_hturn, s_ht, s_down, s_y = (
            sem(f"s_{n}") for n in ("xturn", "xt", "up", "silu", "hid", "hturn", "ht", "down", "y"))
        s_pad2, s_stat = sem("s_pad2"), sem("s_stat")
        s_sum, s_var, s_rstd, s_norm = (sem(f"s_{n}") for n in ("sum", "var", "rstd", "norm"))
        s_out = [sem(f"s_out{n}") for n in range(2)]
        turn_ps, hturn_ps, down_ps = pb[0], pb[1], pb[2]
        g_ps, u_ps = pb[3:5], pb[5:7]
        n_route = 0

        def attention_done(eng):
            for st, last in ((pe, "router"), (act, "logits"), (pool, "ctx"), (dve, "ln_shift")):
                eng.wait_ge(st.sem, st.value(last, POST_ONLY, NW))

        def route(eng):
            v, n = nc.vector, 0

            def link(ins):
                nonlocal n
                n += 1
                ins.then_inc(s_route, 1)
                eng.wait_ge(s_route, n)

            def over_t(x):
                return x.unsqueeze(2).to_broadcast([P, NT, E])

            def over_e(x):
                return x.unsqueeze(1).to_broadcast([P, NT, E])
            link(v.tensor_reduce(top[:, :], logits[:, :, :], AX, ALU.max))
            link(v.tensor_tensor(cand[:, :, :], logits[:, :, :], over_t(top[:, :]), ALU.is_equal))
            link(v.scalar_tensor_tensor(cand[:, :, :], cand[:, :, :], -float(E), over_e(iota_e[:, :]), ALU.mult, ALU.add))
            link(v.tensor_reduce(top[:, :], cand[:, :, :], AX, ALU.min))
            link(v.tensor_tensor(one_hot[:, :, :], cand[:, :, :], over_t(top[:, :]), ALU.is_equal))
            eng.wait_ge(s_count, 2)
            link(v.tensor_copy(total[:, :, :].rearrange("p t e -> p (t e)"), pb[1][:, 0:NT * E]))
            for e in range(E):
                link(v.tensor_tensor_scan(before[:, :, e], ones[:, 0:NT], total[:, :, e], 0.0, ALU.mult, ALU.add))
            link(v.tensor_scalar(tiles_f[:, :], before[:, NT - 1, :], float(P - 1), None, ALU.add))
            link(v.tensor_copy(tiles_i[:, :], tiles_f[:, :]))
            link(v.tensor_scalar(tiles_i[:, :], tiles_i[:, :], P.bit_length() - 1, None, ALU.logical_shift_right))
            link(v.tensor_copy(tiles_f[:, :], tiles_i[:, :]))
            link(v.tensor_tensor_scan(tile_end[:, :], ones[:, 0:E], tiles_f[:, :], 0.0, ALU.mult, ALU.add))
            link(v.tensor_tensor(tiles_f[:, :], tile_end[:, :], tiles_f[:, :], ALU.subtract))
            link(v.tensor_scalar(tiles_f[:, :], tiles_f[:, :], float(P), None, ALU.mult))
            link(v.tensor_tensor(before[:, :, :], before[:, :, :], total[:, :, :], ALU.subtract))
            link(v.tensor_tensor(before[:, :, :], before[:, :, :], over_e(tiles_f[:, :]), ALU.add))
            link(v.tensor_tensor(before[:, :, :], pb[0][:, 0:NT * E].rearrange("p (t e) -> p t e", e=E), before[:, :, :], ALU.add))
            link(v.tensor_tensor(before[:, :, :], before[:, :, :], one_hot[:, :, :], ALU.mult))
            link(v.tensor_reduce(place_f[:, :], before[:, :, :], AX, ALU.add))
            link(v.tensor_copy(place[:, :], place_f[:, :]))
            link(v.tensor_tensor(past[:, :, :], tile_end[0:1, :].unsqueeze(1).to_broadcast([1, MT, E]),
                                 iota_t[:, :].unsqueeze(2).to_broadcast([1, MT, E]), ALU.is_le))
            link(v.tensor_reduce(expert_f[:, :], past[:, :, :], AX, ALU.add))
            link(v.tensor_scalar(expert_f[:, :], expert_f[:, :], float(E - 1), None, ALU.min))
            link(v.tensor_copy(expert_at[:, :], expert_f[:, :]))
            return n

        n_route_hot, n_route_all = 5, 23 + E

        def sorted_tiles(eng, stage):
            for u in range(U):
                stage(0, u, True)
            with eng.Fori(1, MT // U - 1) as i:
                for u in range(U):
                    stage(i, u, True)
            for u in range(U):
                stage(MT // U - 1, u, u < U - 1)

        def token_windows(eng, stage):
            for par in range(2):
                stage(0, par)
            with eng.Fori(1, NW // 2) as i:
                for par in range(2):
                    stage(i, par)

        def at_least(eng, s, value):
            if not isinstance(value, int) or value > 0:
                eng.wait_ge(s, value)

        def finish_sync(eng):
            attention_done(eng)
            eng.dma_start(gate_we[:, :, :], t["gate_w"]).then_inc(s_wexp, 16)
            eng.dma_start(up_we[:, :, :], t["up_w"]).then_inc(s_wexp, 16)
            eng.dma_start(down_we[:, :, :, :], t["down_w"]).then_inc(s_wexp, 16)
            eng.wait_ge(s_sorted, 16 * NT)

            def load(tile, u):
                eng.dma_start(xs[u][:, :], t["x_sorted"][bass.ds(tile * P, P), :]).then_inc(s_xs[u], 16)
            for u in range(U):
                load(u, u)

            def stage(i, u, more):
                tile = i * U + u
                eng.wait_ge(s_y, tile + 1)
                eng.dma_start(t["y_sorted"][bass.ds(tile * P, P), :], ys[u][:, :]).then_inc(s_ys[u], 16)
                if not isinstance(i, int) or i == 0:
                    eng.wait_ge(s_xturn, tile + 1)
                    load(tile + U, u)
            sorted_tiles(eng, stage)

            def out(i, par):
                eng.wait_ge(s_norm, 4 * (i * 2 + par) + 4)
                eng.dma_start(t["out"][bass.ds(i * 2 + par, 1), :, :].rearrange("o p n -> (o p) n"),
                              out_y[par][:, :, :].rearrange("p i d -> p (i d)")).then_inc(s_out[par], 16)
            token_windows(eng, out)
            for par in range(2):
                eng.wait_ge(s_out[par], 16 * (NW // 2))

        def finish_pe(eng):
            attention_done(eng)
            mm, tr = nc.tensor.matmul, nc.tensor.transpose
            eng.wait_ge(s_route, n_route_hot)
            hot = one_hot[:, :, :].rearrange("p t e -> p (t e)")
            mm(pb[0][:, 0:NT * E], below[:, :], hot, start=True, stop=True).then_inc(s_count, 1)
            mm(pb[1][:, 0:NT * E], ones[:, :], hot, start=True, stop=True).then_inc(s_count, 1)
            eng.wait_ge(s_route, n_route_all)
            eng.wait_ge(s_wexp, 48)

            def x_turn(i, u):
                tile = i * U + u
                eng.wait_ge(s_xs[u], (i + 1) * 16)
                at_least(eng, s_xt, tile)
                tr(turn_ps[:, 0:P], xs[u][:, :], ident[:, :]).then_inc(s_xturn, 1)

            def gate_up(i, u):
                tile, par = i * U + u, u % 2
                at = eng.value_load(expert_at[0:1, bass.ds(tile, 1)], min_val=0, max_val=E - 1) * I
                eng.wait_ge(s_xt, tile + 1)
                at_least(eng, s_hid, tile - 1)
                for ps, we in ((g_ps, gate_we), (u_ps, up_we)):
                    mm(ps[par][:, 0:I], xs_t[par][:, :], we[:, :, :].rearrange("p e i -> p (e i)")[:, bass.ds(at, I)],
                       start=True, stop=True).then_inc(s_up, 1)

            def h_turn(i, u):
                tile, par = i * U + u, u % 2
                eng.wait_ge(s_hid, tile + 1)
                at_least(eng, s_ht, tile)
                for c in range(IC):
                    last = tr(hturn_ps[:, c * P:(c + 1) * P], hid[par][:, c * P:(c + 1) * P], ident[:, :])
                last.then_inc(s_hturn, 1)

            def down(i, u):
                tile, par = i * U + u, u % 2
                at = eng.value_load(expert_at[0:1, bass.ds(tile, 1)], min_val=0, max_val=E - 1) * D
                eng.wait_ge(s_ht, tile + 1)
                at_least(eng, s_y, tile)
                for c in range(IC):
                    last = mm(down_ps[:, 0:D], hid_t[par][:, c, :],
                              down_we[:, c, :, :].rearrange("p e d -> p (e d)")[:, bass.ds(at, D)],
                              start=(c == 0), stop=(c == IC - 1))
                last.then_inc(s_down, 1)

            def stage(i, u, more):
                j, w = (i, u + 1) if u < U - 1 else (i + 1, 0)
                if more:
                    x_turn(j, w)
                h_turn(i, u)
                if more:
                    gate_up(j, w)
                down(i, u)
            x_turn(0, 0)
            gate_up(0, 0)
            sorted_tiles(eng, stage)

        def finish_act(eng):
            attention_done(eng)
            A = nc.scalar.activation

            def x_copy(i, u):
                tile, par = i * U + u, u % 2
                eng.wait_ge(s_xturn, tile + 1)
                at_least(eng, s_up, 2 * tile - 2)
                A(xs_t[par][:, :], turn_ps[:, 0:P], ACT.Copy).then_inc(s_xt, 1)

            def silu_of(i, u):
                tile, par = i * U + u, u % 2
                eng.wait_ge(s_up, 2 * tile + 1)
                at_least(eng, s_hid, tile - 1)
                A(silu[par][:, :], g_ps[par][:, 0:I], ACT.Silu).then_inc(s_silu, 1)

            def h_copy(i, u):
                tile, par = i * U + u, u % 2
                eng.wait_ge(s_hturn, tile + 1)
                at_least(eng, s_down, tile - 1)
                A(hid_t[par][:, :, :].rearrange("p c n -> p (c n)"), hturn_ps[:, 0:IC * P], ACT.Copy).then_inc(s_ht, 1)

            def stage(i, u, more):
                j, w = (i, u + 1) if u < U - 1 else (i + 1, 0)
                if more:
                    x_copy(j, w)
                h_copy(i, u)
                if more:
                    silu_of(j, w)
            x_copy(0, 0)
            silu_of(0, 0)
            sorted_tiles(eng, stage)

            def norm(i, par):
                w = i * 2 + par
                eng.wait_ge(s_var, TW * (w + 1))
                A(rstd[:, :], mv[:, :, 1], ACT.Ln, bias=ln_eps[:, 0:1]).then_inc(s_rstd, 1)
                eng.wait_ge(s_rstd, 2 * w + 1)
                A(rstd[:, :], rstd[:, :], ACT.Exp, scale=-0.5).then_inc(s_rstd, 1)
            token_windows(eng, norm)

        def finish_pool(eng):
            attention_done(eng)
            eng.wait_ge(s_pad, 16)
            eng.wait_ge(s_route, n_route_all)

            def index(m):
                return bass.IndirectOffsetOnAxis(ap=place[:, m:m + 1], axis=0)
            for m in range(NT):
                eng.indirect_dma_start(t["x_sorted"], index(m), x1_all[:, m, :], None).then_inc(s_sorted, 16)
            for u in range(U):
                eng.wait_ge(s_ys[u], 16 * (MT // U))
            for w in range(NW):
                if w >= 2:
                    eng.wait_ge(s_sum, w - 1)
                for i in range(TW):
                    eng.indirect_dma_start(back_y[w % 2][:, i, :], None, t["y_sorted"], index(w * TW + i)) \
                        .then_inc(s_back[w % 2], 16)

        def finish_dve(eng):
            attention_done(eng)
            v = nc.vector
            assert route(eng) == n_route_all
            for par in range(2):
                v.memset(hid[par][:, I:IC * P], 0.0).then_inc(s_pad2, 1)
            eng.wait_ge(s_pad2, 2)

            def hidden(i, u):
                tile, par = i * U + u, u % 2
                eng.wait_ge(s_silu, tile + 1)
                eng.wait_ge(s_up, 2 * tile + 2)
                at_least(eng, s_hturn, tile - 1)
                v.tensor_tensor(hid[par][:, 0:I], u_ps[par][:, 0:I], silu[par][:, :], ALU.mult).then_inc(s_hid, 1)

            def y_copy(i, u):
                eng.wait_ge(s_down, i * U + u + 1)
                at_least(eng, s_ys[u], i * 16)
                v.tensor_copy(ys[u][:, :], down_ps[:, 0:D]).then_inc(s_y, 1)

            def stage(i, u, more):
                j, w = (i, u + 1) if u < U - 1 else (i + 1, 0)
                if more:
                    hidden(j, w)
                y_copy(i, u)
            hidden(0, 0)
            sorted_tiles(eng, stage)

            def norm(i, par):
                w = i * 2 + par
                eng.wait_ge(s_back[par], 16 * TW * (i + 1))
                v.tensor_tensor(res_y[par][:, :, :], back_y[par][:, :, :], x1_all[:, bass.ds(w * TW, TW), :], ALU.add) \
                    .then_inc(s_sum, 1)
                eng.wait_ge(s_sum, w + 1)
                for k in range(TW):
                    v.bn_stats(stats[:, k, :], res_y[par][:, k, :]).then_inc(s_stat, 1)
                eng.wait_ge(s_stat, TW * (w + 1))
                v.tensor_copy(settle[:, :], ones[:, 0:1])
                for k in range(TW):
                    v.bn_aggr(mv[:, k, :], stats[:, k, :]).then_inc(s_var, 1)
                eng.wait_ge(s_rstd, 2 * w + 2)
                at_least(eng, s_out[par], 16 * i)
                for k in range(TW):
                    v.tensor_scalar(out_y[par][:, k, :], res_y[par][:, k, :], mv[:, k, 0:1], rstd[:, k:k + 1],
                                    ALU.subtract, ALU.mult).then_inc(s_norm, 1)
                eng.wait_ge(s_norm, TW * (w + 1))
            token_windows(eng, norm)

        block = ctx.enter_context(nc.Block())

        def slots(tile):
            return tile.rearrange("p (n j) -> p j n", j=C)

        def chunk_jb(tile, c):
            return tile.rearrange("p (b c j) -> p c j b", c=NCH, j=C)[:, c, :, :]

        def slot_chunk(tile, c):
            return tile[:, :, :].rearrange("p s (b c) -> p c s b", c=NCH)[:, c, :, :]

        def rep_chunk(tile, c, order):
            return tile[:, :, :].rearrange("p d (b c j) -> p c d b j", c=NCH, j=C)[:, c, :, :, :] \
                .rearrange(f"p d b j -> p {order}")

        links = ["k_prod", "k_sum", "decay", "k_gam", "rhs"]
        links += [f"{m}{j}" for j in range(C - 1) for m in ("tri", "sub")] + ["d_end", "upd", "S"]
        s_link = {(name, h): sem(f"s_{name}_{h}") for name in links for h in range(2)}

        class Body:

            def __init__(self, steps, eng, kind, win, dry):
                self.steps, self.eng, self.kind, self.win, self.dry = steps, eng, kind, win, dry
                if dry:
                    steps.order[kind] = []
                self.at = 0

            def step(self, label, ins):
                if self.dry:
                    self.steps.order[self.kind].append(label)
                else:
                    assert self.steps.order[self.kind][self.at] == label
                    ins().then_inc(self.steps.sem, 1)
                self.at += 1

            def wait(self, steps, label, back=0):
                if self.dry:
                    return
                kind, body = self.kind, self.win.w
                if back:
                    n = body if isinstance(body, int) else None
                    if n is None:
                        kind = FULL
                    else:
                        m = n - back
                        kind = PRE_ONLY if m == -1 else FIRST if m == 0 else LAST if m == NW - 1 else FULL
                        if m < -1:
                            return
                if label not in steps.order[kind]:
                    return
                self.eng.wait_ge(steps.sem, steps.value(label, kind, body - back))

            def link(self, name, c, back=0):
                w = self.win.w - back
                if self.dry or (isinstance(w, int) and not 0 <= w < NW):
                    return
                for h in range(2):
                    self.eng.wait_ge(s_link[name, h], w * NCH + c + 1)

            def own(self):
                if self.dry or not self.at:
                    return
                label = self.steps.order[self.kind][self.at - 1]
                self.eng.wait_ge(self.steps.sem, self.steps.value(label, self.kind, self.win.w))

            def dma(self, sems, win, per=16):
                if not self.dry:
                    self.eng.wait_ge(sems[win.par], (win.i + 1) * per)

            def dma1(self, s, win, per=16):
                if not self.dry:
                    self.eng.wait_ge(s, (win.w + 1) * per)

        def pe_body(b):
            w = b.win
            pre, chain, post = HAS_PRE[b.kind], HAS_CHAIN[b.kind], HAS_POST[b.kind]
            nxt, prv = w.shift(1), w.shift(-1)
            mm, tr = nc.tensor.matmul, nc.tensor.transpose

            def project(label, n, out, bias=False):
                def go():
                    if bias:
                        mm(out, dt_row[:, :], ones[0:1, :].unsqueeze(1).to_broadcast([1, TW, P]), start=True, stop=False)
                    return mm(out, w_proj[:, n, :], x_ct[nxt.par][:, :], start=not bias, stop=True)
                b.step(label, go)

            def head_sum(label, src, out, ready, by=heads):
                b.wait(*ready)
                b.step(label, lambda: mm(out[:, 0:src.shape[1]], by[:, :], src, start=True, stop=True))

            def y_chunks(m, win, back=0):
                b.wait(pool, f"q_prod{2 * m + 1}", back)
                if m == 0:
                    b.wait(act, "y_sq", back=1)
                    b.wait(dve, "y_n", back=1)
                out = y_ps[win.par].rearrange("p (j b c) -> p c j b", j=C, c=NCH)[:, 2 * m:2 * m + 2, :, :]

                def go():
                    for d in range(DH):
                        i = mm(out, ident[:, :], q_prod[m][:, d, :, :, :], start=(m == 0 and d == 0), stop=(d == DH - 1),
                               skip_group_check=True)
                    return i
                b.step(f"y{m}", go)

            def y_deltas():
                b.wait(pool, "y_prod3")
                y = y_ps[prv.par].rearrange("p (j n) -> p j n", j=C)

                def go():
                    at = 0
                    for d in range(C):
                        i = mm(y[:, d:C, :], ident[:, :], y_prod[:, at:at + C - d, :], start=False, stop=True,
                               skip_group_check=True)
                        at += C - d
                    return i
                b.step("y", go)

            def soft_sum(n, label):
                if n == 0:
                    b.wait(act, "zbg_ln")
                if n == 2:
                    b.wait(act, "gate_g")

                def go():
                    mm(zbg_ps[:, n, :], ident[:, :], zbg_r[:, n, :], start=True, stop=False)
                    return mm(zbg_ps[:, n, :], ident[:, :], zbg_a[:, n, :], start=False, stop=True)
                b.step(label, go)

            def y_mean():
                b.wait(act, "y_sq")
                b.wait(act, "logits", back=1)
                b.step("ms", lambda: mm(post_ps, heads_mean[:, :], y_sq[:, :], start=True, stop=True))

            def out_proj():
                if not b.dry:
                    b.dma(s_xtc, prv)
                b.wait(act, "rms")
                b.step("res", lambda: mm(post_ps, ident[:, :], x_tc[:, :], start=True, stop=False, skip_group_check=True))
                b.wait(pool, "ctx")

                def go():
                    mm(post_ps, ones[0:1, :], bias_o[0:1, :].unsqueeze(1).to_broadcast([1, TW, D]), start=False, stop=False, skip_group_check=True)
                    for i in range(TW):
                        last = mm(post_ps[:, i * D:(i + 1) * D], ctx_t[:, i * P:(i + 1) * P], w_o[:, :],
                                  start=False, stop=True, skip_group_check=True)
                    return last
                b.step("attn", go)

            def turn():
                b.wait(act, f"x1_{TW - 1}")

                def go():
                    for i in range(TW):
                        last = tr(post_ps[:, i * P:(i + 1) * P], x1[:, i, :], ident[:, :])
                    return last
                b.step("turn", go)

            def router():
                b.wait(act, "x1_ct")

                def go():
                    for i in range(TW):
                        last = mm(post_ps[:, i * E:(i + 1) * E], x1_ct[:, i, :], w_r[:, :], start=True, stop=True)
                    return last
                b.step("router", go)

            qkf = qk[:, :, :].rearrange("p s n -> p (s n)")
            kkf = kk.rearrange("p s n -> p (s n)")
            if pre:
                if not b.dry:
                    b.dma(s_xct, nxt)
                b.wait(dve, "aqk_far", back=1)
                b.wait(act, "aqk_same", back=1)
                project("z", 5, zbg_ps[:, 0, :], True)
                project("b", 4, zbg_ps[:, 1, :])
                project("g", 3, zbg_ps[:, 2, :])
                b.wait(dve, "akk_far", back=1)
                project("k", 1, kq_ps[:, 0, :])
                project("q", 0, kq_ps[:, 1, :])
            if post:
                y_chunks(2, prv, back=1)
            if pre:
                b.wait(act, "kq_s")
                head_sum("nk", kq_sq[:, 0, :], kq_ps[:, 0, :], (act, "kq_sq"))
                head_sum("nq", kq_sq[:, 1, :], kq_ps[:, 1, :], (act, "kq_sq"), heads_q)
            if post:
                y_chunks(3, prv, back=1)
            if pre:
                soft_sum(0, "z_sum")
                soft_sum(1, "b_sum")
                soft_sum(2, "g_sum")
                b.wait(act, "alpha")
                project("v", 2, zbg_ps[:, 0, :])
            if post:
                y_deltas()
                y_mean()
            if chain:
                y_chunks(0, w)
            if post:
                out_proj()
            if chain:
                y_chunks(1, w)
            if pre:
                b.wait(act, "g_sig")
                b.wait(dve, "beta_v")
                head_sum("qk_same", qkf[:, 0:4 * NN], zbg_ps[:, 0, :], (pool, "qk_same"))
                head_sum("qk_near", qkf[:, 4 * NN:7 * NN], zbg_ps[:, 1, :], (pool, "qk_near"))
            if pre:
                head_sum("qk_far", qkf[:, 7 * NN:10 * NN], zbg_ps[:, 2, :], (pool, "qk_far2"))
            if pre:
                b.wait(act, "kq_ln")
                head_sum("kk_near", kkf[:, 0:3 * NN], kq_ps[:, 0, :], (pool, "kk_near"))
                head_sum("kk_far", kkf[:, 3 * NN:6 * NN], kq_ps[:, 1, :], (pool, "kk_far2"))
            if post:
                turn()
                router()

        def act_body(b):
            w = b.win
            pre, post = HAS_PRE[b.kind], HAS_POST[b.kind]
            nxt, prv = w.shift(1), w.shift(-1)
            A = nc.scalar.activation

            if pre:
                b.wait(pool, "beta_gam", back=1)
                b.wait(dve, "akk_far", back=1)
                b.wait(pe, "qk_far", back=1)
                b.wait(act, "to_end2", back=1)
                if not b.dry and not (isinstance(w.w, int) and w.w < 0):
                    b.dma1(s_kout, w)
                    b.dma1(s_qout, w)
                b.wait(pe, "g")
                b.step("zbg_relu", lambda: A(zbg_r[:, :, :], zbg_ps, ACT.Relu, scale=-1.0))
                b.step("zbg_abs", lambda: A(zbg_a[:, :, :], zbg_ps, ACT.Abs))
                b.wait(pe, "q")
                b.step("kq_sq", lambda: A(kq_sq[:, :, :], kq_ps, ACT.Square))
                b.step("kq_s", lambda: A(kq_s[:, :, :], kq_ps, ACT.Copy))
                b.wait(act, "zbg_abs")
                b.step("zbg_exp", lambda: A(zbg_a[:, :, :], zbg_a[:, :, :], ACT.Exp, scale=-1.0))
                b.own()
                b.step("zbg_ln", lambda: A(zbg_a[:, :, :], zbg_a[:, :, :], ACT.Ln, bias=1.0))
                b.wait(pe, "nq")
                b.step("kq_ln", lambda: A(kq_sq[:, :, :], kq_ps, ACT.Ln))
                b.own()
                b.step("kq_r", lambda: A(kq_sq[:, :, :], kq_sq[:, :, :], ACT.Exp, scale=-0.5))
                b.step("gate_g", lambda: A(gate_in[:, :], zbg_ps[:, 2, :], ACT.Copy, scale=norm_w[:, 0:1]))
            if pre:
                b.wait(pe, "z_sum")
                b.step("alpha", lambda: A(alpha, zbg_ps[:, 0, :], ACT.Exp, scale=neg_a[:, 0:1]))
                b.wait(pe, "b_sum")
                b.step("beta", lambda: A(beta, zbg_ps[:, 1, :], ACT.Exp, scale=-1.0))
                b.wait(pe, "g_sum")
                b.step("g_sig", lambda: A(g_sig, zbg_ps[:, 2, :], ACT.Exp, scale=-1.0))
                b.link("S", NCH - 1, back=1)
                b.wait(act, "alpha")
                b.step("gam0", lambda: A(slots(gam[nxt.par])[:, 0, :], slots(alpha)[:, 0, :], ACT.Copy))
                b.step("to_end2", lambda: A(to_end[nxt.par][:, 2, :], slots(alpha)[:, 3, :], ACT.Copy))
            if post:
                b.wait(pe, "y")
                b.wait(dve, "y_n", back=1)
                b.wait(pe, "router", back=1)
                b.step("y_sq", lambda: A(y_sq[:, :], y_ps[prv.par], ACT.Square))
                b.wait(pe, "ms")
                b.step("rms", lambda: A(y_sq[:, :], post_ps, ACT.Ln, bias=rms_eps[:, 0:1]))
                b.own()
                b.step("rms_r", lambda: A(y_sq[:, :], y_sq[:, :], ACT.Exp, scale=-0.5))
            if pre:
                b.wait(pool, "far2")
                b.step("to_end1", lambda: A(to_end[nxt.par][:, 1, :], far[:, 1, :], ACT.Copy))
                b.step("to_end0", lambda: A(to_end[nxt.par][:, 0, :], far[:, 2, :], ACT.Copy))
            if pre:
                b.wait(pe, "qk_same")
                b.step("aqk_same", lambda: A(aqk[nxt.par][:, 0:4, :].rearrange("p s n -> p (s n)"), zbg_ps[:, 0, :], ACT.Copy))
            if post:
                b.wait(dve, f"mv{TW - 1}")
                b.wait(act, f"x1_{TW - 1}", back=1)
                b.step("ln_ln", lambda: A(rstd[:, :], mv[:, :, 1], ACT.Ln, bias=ln_eps[:, 0:1]))
                b.own()
                b.step("ln_r", lambda: A(rstd[:, :], rstd[:, :], ACT.Exp, scale=-0.5))
                b.wait(dve, "ln_shift")
                b.wait(pool, "ctx")
                b.wait(pe, "turn", back=1)
                b.wait(act, "x1_keep", back=1)
                for i in range(TW):
                    b.step(f"x1_{i}", lambda: A(x1[:, i, :], post_ps[:, i * D:(i + 1) * D], ACT.Identity,
                                                bias=shift[:, i:i + 1], scale=rstd[:, i:i + 1]))
                b.wait(dve, "y_n")
                at = prv.w * TW
                b.own()
                b.step("x1_keep", lambda: A(x1_all[:, bass.ds(at, TW), :], x1[:, :, :], ACT.Copy))
                b.wait(pe, "turn")
                b.step("x1_ct", lambda: A(x1_ct, post_ps.rearrange("p (i n) -> p i n", i=TW), ACT.Copy))
            if post:
                b.wait(pe, "router")
                b.step("logits", lambda: A(logits[:, bass.ds(at, TW), :],
                                           post_ps[:, 0:TW * E].rearrange("p (i e) -> p i e", i=TW), ACT.Copy))

        def pool_body(b):
            w = b.win
            pre, chain, post = HAS_PRE[b.kind], HAS_CHAIN[b.kind], HAS_POST[b.kind]
            nxt, prv = w.shift(1), w.shift(-1)
            tt = nc.gpsimd.tensor_tensor

            def mul(label, out, x, y, op=ALU.mult):
                b.step(label, lambda: tt(out, x, y, op))

            def q_times_s(c):
                if c == 0:
                    if not b.dry:
                        b.dma(s_qrep, w)
                    b.link("S", NCH - 1, back=1)
                else:
                    b.link("S", c - 1)
                if c % 2 == 0:
                    last, back = (("y0", 1), ("y3", 0), ("y2", 0), ("y1", 0))[c // 2]
                    b.wait(pe, last, back)
                s = S[c % NS][:, :, :].rearrange("p b d -> p d b").unsqueeze(2).to_broadcast([P, DH, C, NB])
                mul(f"q_prod{c}", q_prod[c // 2][:, :, c % 2, :, :], s, rep_chunk(q_rep[w.par], c, "d j b"))

            if post:
                b.link("sub2", NCH - 1, back=1)
                b.wait(pe, "qk_far", back=1)
                dl, aq, at = delta[prv.par], aqk[prv.par], 0
                for d in range(C):
                    mul(f"y_prod{d}", y_prod[:, at:at + C - d, :], aq[:, at:at + C - d, :], dl[:, 0:C - d, :])
                    at += C - d
            if chain:
                q_times_s(0)
                q_times_s(1)
            if pre:
                b.wait(act, "kq_r")
                mul("kq_n", kq_s[:, :, :], kq_s[:, :, :], kq_sq[:, :, :])
            if chain:
                q_times_s(2)
            if pre:
                al, bt = slots(alpha), slots(beta)
                gm = slots(gam[nxt.par])
                b.wait(act, "gam0")
                mul("far0", far[:, 0:2, :], al[:, 2:4, :], al[:, 1:3, :])
                mul("gam1", gm[:, 1, :], al[:, 0, :], al[:, 1, :])
                b.own()
                mul("far2", far[:, 2, :], far[:, 1, :], al[:, 1, :])
                mul("gam2", gm[:, 2, :], gm[:, 1, :], al[:, 2, :])
                b.own()
                mul("gam3", gm[:, 3, :], gm[:, 2, :], al[:, 3, :])
                b.own()
                mul("q_gam", q_scaled, q_s, gam[nxt.par][:, :])
                kn, qn = slots(k_s), slots(q_s)
                b.wait(pe, "y")
                mul("qk_same", qk[:, 0:4, :], qn, kn)
            if post:
                b.wait(dve, "y_n")
                b.wait(pe, "attn", back=1)
                mul("ctx", slots(ctx_t[:, :]), y_n.rearrange("p (j n) -> p j n", j=C), slots(gate[prv.par][:, :]))
            if pre:
                mul("qk_near", qk[:, 4:7, :], qn[:, 1:4, :], kn[:, 0:3, :])
                mul("qk_far", qk[:, 7:9, :], qn[:, 2:4, :], kn[:, 0:2, :])
                mul("qk_far2", qk[:, 9, :], qn[:, 3, :], kn[:, 0, :])
            if chain:
                q_times_s(3)
            if pre:
                b.wait(pe, "g_sum")
                mul("kk_near", kk[:, 0:3, :], kn[:, 1:4, :], kn[:, 0:3, :])
                mul("kk_far", kk[:, 3:5, :], kn[:, 2:4, :], kn[:, 0:2, :])
                mul("kk_far2", kk[:, 5, :], kn[:, 3, :], kn[:, 0, :])
                b.wait(act, "beta")
                mul("beta_near", beta_near, bt[:, 1:4, :], al[:, 1:4, :])
                mul("beta_far", beta_far[:, 0:2, :], bt[:, 2:4, :], far[:, 0:2, :])
                mul("beta_far2", beta_far[:, 2, :], bt[:, 3, :], far[:, 2, :])
                b.wait(act, "g_sig")
                b.wait(pool, "ctx")
                mul("gate", gate[nxt.par][:, :], gate_in[:, :], g_sig)
            if chain:
                q_times_s(4)
            if pre:
                mul("beta_gam", beta_gam[nxt.par][:, :], beta, gam[nxt.par][:, :])
            if chain:
                q_times_s(5)
            if chain:
                q_times_s(6)
            if chain:
                q_times_s(7)

        def dve_body(b):
            w = b.win
            pre, chain, post = HAS_PRE[b.kind], HAS_CHAIN[b.kind], HAS_POST[b.kind]
            nxt, prv = w.shift(1), w.shift(-1)
            v = nc.vector
            HB = NB // 2

            def r3(bank):
                return bank[:, 0:3 * NN].rearrange("p (s n) -> p s n", s=3)

            def half_chunk(c, h):
                bs = slice(h * HB, (h + 1) * HB)
                kr, dl = k_rep[w.par], slot_chunk(delta[w.par], c)[:, :, bs]
                s_in, s_out = S[c % NS][:, bs, :], S[(c + 1) % NS][:, bs, :]
                up, ks_h, tri_h, de = upd[:, bs, :, :], ks[:, :, bs], tri[:, :, bs], d_end[:, :, bs]
                n = C * HB * DH
                at = h * HB * DH * (C + 1)
                flat = upd[:, :, :, :].rearrange("p b d s -> p (b d s)")[:, at:at + n]
                prod = flat.rearrange("p (j b d) -> p j b d", j=C, b=HB)

                def rep(order):
                    return k_rep[w.par][:, :, :].rearrange("p d (b c j) -> p c d b j", c=NCH, j=C)[:, c, :, bs, :] \
                        .rearrange(f"p d b j -> p {order}")
                yield "k_prod", lambda: v.tensor_tensor(
                    prod, s_in.unsqueeze(1).to_broadcast([P, C, HB, DH]), rep("j b d"), ALU.mult)
                yield "k_sum", lambda: v.tensor_reduce(ks_h, prod, AX, ALU.add)
                yield "decay", lambda: v.tensor_tensor(
                    up[:, :, :, C], s_in,
                    chunk_jb(gam[w.par][:, :], c)[:, C - 1, bs].unsqueeze(2).to_broadcast([P, HB, DH]), ALU.mult)
                yield "k_gam", lambda: v.tensor_tensor(ks_h, ks_h, chunk_jb(beta_gam[w.par][:, :], c)[:, :, bs], ALU.mult)
                yield "rhs", lambda: v.tensor_tensor(dl, chunk_jb(beta_v[w.par][:, :], c)[:, :, bs], ks_h, ALU.subtract)
                for s in range(C - 1):
                    m = C - 1 - s
                    a = slot_chunk(akk[w.par], c)[:, s:s + C * (m - 1) + 1:C, bs]
                    yield f"tri{s}", lambda: v.tensor_tensor(
                        tri_h[:, 0:m, :], a, dl[:, s:s + 1, :].to_broadcast([P, m, HB]), ALU.mult)
                    yield f"sub{s}", lambda: v.tensor_tensor(dl[:, s + 1:C, :], dl[:, s + 1:C, :], tri_h[:, 0:m, :], ALU.subtract)
                yield "d_end", lambda: v.tensor_tensor(de, dl, slot_chunk(to_end[w.par], c)[:, :, bs], ALU.mult)
                yield "upd", lambda: v.tensor_tensor(
                    up[:, :, :, 0:C], rep("b d j"),
                    de.rearrange("p j b -> p b j").unsqueeze(2).to_broadcast([P, HB, DH, C]), ALU.mult)
                yield "S", lambda: v.tensor_reduce(s_out, up, AX, ALU.add)

            def chunk(c):
                if c == 0:
                    if not b.dry:
                        b.dma(s_krep, w)
                    b.wait(pool, "beta_gam", back=1)
                    b.wait(act, "to_end0", back=1)
                    b.wait(pool, "y_prod3", back=1)
                    b.wait(dve, "akk_far", back=1)
                    b.wait(dve, "beta_v", back=1)
                before, done = w.w * NCH + c, w.w * NCH + c + 1
                if not isinstance(before, int) and not b.dry:
                    before, done = b.eng.to_reg(before), b.eng.to_reg(done)
                for k, pair in enumerate(zip(half_chunk(c, 0), half_chunk(c, 1))):
                    for h, (name, ins) in enumerate(pair):
                        assert name == links[k]
                        if name == "S":
                            b.wait(pool, f"q_prod{(c + 1 - NS) % NCH}", back=0 if c + 1 >= NS else 1)
                        if b.dry:
                            continue
                        if k:
                            b.eng.wait_ge(s_link[links[k - 1], h], done)
                        elif not isinstance(before, int) or before > 0:
                            b.eng.wait_ge(s_link["S", h], before)
                        ins().then_inc(s_link[name, h], 1)

            if chain:
                chunk(0)
                chunk(1)
                chunk(2)
                chunk(3)
            if pre:
                b.wait(act, "beta")
                b.wait(pe, "v")
                b.link("rhs", NCH - 1, back=1)
                b.step("beta_v", lambda: v.tensor_tensor(beta_v[nxt.par][:, :], zbg_ps[:, 0, :], beta, ALU.mult))
            if post:
                b.wait(act, "rms_r")
                b.wait(pe, "y")
                b.wait(act, "x1_keep", back=1)
                b.wait(pe, "turn", back=1)
                b.step("y_n", lambda: v.tensor_tensor(y_n, y_ps[prv.par], y_sq[:, :], ALU.mult))
            if chain:
                chunk(4)
            if post:
                b.wait(pe, "attn")
                b.wait(act, "ln_ln", back=1)
                for i in range(TW):
                    b.step(f"stats{i}", lambda: v.bn_stats(stats[:, i, :], post_ps[:, i * D:(i + 1) * D]))
                b.own()
                b.step("settle", lambda: v.tensor_copy(settle[:, :], ones[:, 0:1]))
                for i in range(TW):
                    b.step(f"mv{i}", lambda: v.bn_aggr(mv[:, i, :], stats[:, i, :]))
            if chain:
                chunk(5)
            if post:
                b.wait(act, "ln_r")
                b.wait(act, f"x1_{TW - 1}", back=1)
                b.step("ln_shift", lambda: v.scalar_tensor_tensor(shift[:, :], mv[:, :, 0], -1.0, rstd[:, :], ALU.mult, ALU.mult))
            if pre:
                aq = aqk[nxt.par]
                b.wait(pe, "qk_near")
                b.wait(pool, "y_prod3")
                b.step("aqk_near", lambda: v.tensor_tensor(aq[:, 4:7, :], r3(zbg_ps[:, 1, :]), slots(alpha)[:, 1:4, :], ALU.mult))
                b.wait(pe, "qk_far")
                b.step("aqk_far", lambda: v.tensor_tensor(aq[:, 7:10, :], r3(zbg_ps[:, 2, :]), far[:, :, :], ALU.mult))
            if chain:
                chunk(6)
            if pre:
                ak = akk[nxt.par]
                near, away = r3(kq_ps[:, 0, :]), r3(kq_ps[:, 1, :])
                b.wait(pe, "kk_near")
                b.wait(pool, "beta_far2")
                b.step("akk_near", lambda: v.tensor_tensor(ak[:, 0:3, :], near, beta_near, ALU.mult))
                b.wait(pe, "kk_far")
                b.step("akk_far2", lambda: v.tensor_tensor(ak[:, 8, :], away[:, 2, :], beta_far[:, 2, :], ALU.mult))
                b.step("akk_far", lambda: v.tensor_tensor(ak[:, 4:6, :], away[:, 0:2, :], beta_far[:, 0:2, :], ALU.mult))
            if chain:
                chunk(7)

        def sp_body(b):
            w = b.win
            pre, chain, post = HAS_PRE[b.kind], HAS_CHAIN[b.kind], HAS_POST[b.kind]
            nxt, prv, far2 = w.shift(1), w.shift(-1), w.shift(2)
            e = b.eng
            if chain:
                if not (isinstance(w.w, int) and w.w + 2 >= NW):
                    b.wait(pe, "v", back=1)
                    e.dma_start(x_ct[w.par][:, :], t["x_ct"][:, bass.ds(far2.w, 1), :].rearrange("p o n -> p (o n)")) \
                        .then_inc(s_xct[w.par], 16)
            if pre:
                if not (isinstance(w.w, int) and w.w <= 0):
                    b.dma(s_krep, prv)
                    b.dma(s_qrep, prv)
                b.wait(pool, "kq_n")
                e.dma_start(t["k_dram"][nxt.par], k_s).then_inc(s_kout, 16)
                b.wait(pool, "q_gam")
                e.dma_start(t["q_dram"][nxt.par], q_scaled).then_inc(s_qout, 16)
                for name, dst, s_out, s_rep in (("k_dram", k_rep, s_kout, s_krep), ("q_dram", q_rep, s_qout, s_qrep)):
                    b.dma1(s_out, nxt)
                    src = t[name][nxt.par].rearrange("(h d) n -> h (d n)", d=DH).unsqueeze(1).to_broadcast([H, DH, DH * WN])
                    e.dma_start(dst[nxt.par][:, :, :].rearrange("p d n -> p (d n)"), src).then_inc(s_rep[nxt.par], 16)
            if chain:
                b.wait(pe, "res")
                e.dma_start(x_tc[:, :], t["x_tc"][bass.ds(w.w, 1), :, :].rearrange("o p n -> (o p) n")) \
                    .then_inc(s_xtc[w.par], 16)

        def windows(steps, eng, body, setup):
            def run(kind, win):
                body(Body(steps, eng, kind, win, False))
            setup(eng)
            run(PRE_ONLY, Win(-1, 1))
            run(FIRST, Win(0, 0))
            run(FULL, Win(0, 1))
            with eng.Fori(1, NW // 2 - 1) as i:
                run(FULL, Win(i, 0))
                run(FULL, Win(i, 1))
            run(FULL, Win(NW // 2 - 1, 0))
            run(LAST, Win(NW // 2 - 1, 1))
            run(POST_ONLY, Win(NW // 2, 0))

        for steps, body in ((pe, pe_body), (act, act_body), (pool, pool_body), (dve, dve_body)):
            for kind in range(5):
                body(Body(steps, None, kind, Win(0, 0), True))

        n_const = 16 * (len(t["consts"]) + 4)
        n_setup = 8
        tiles = dict(w_q=w_proj[:, 0, :], w_k=w_proj[:, 1, :], w_v=w_proj[:, 2, :], w_g=w_proj[:, 3, :],
                     w_b=w_proj[:, 4, :], w_a=w_a[:, :], w_o=w_o[:, :], w_r=w_r[:, :], ident=ident[:, :],
                     heads=heads[:, :], heads_q=heads_q[:, :], heads_mean=heads_mean[:, :], below=below[:, :], ones=ones[:, :],
                     iota_e=iota_e[:, :], iota_t=iota_t[:, :])

        @block.sync
        def _(eng):
            def setup(e):
                for name, src in t["consts"].items():
                    e.dma_start(tiles[name], src).then_inc(s_const, 16)
                for n in range(2):
                    e.dma_start(x_ct[n][:, :], t["x_ct"][:, n, :]).then_inc(s_xct[n], 16)
                e.dma_start(dt_in[:, :], t["dt_bias"].rearrange("(o h) -> o h", o=1)).then_inc(s_const, 16)
                e.dma_start(neg_a[:, :], t["A_log"].rearrange("(h o) -> h o", o=1).unsqueeze(1).to_broadcast([H, DH, 1])).then_inc(s_const, 16)
                e.dma_start(norm_w[:, :], t["norm_w"].rearrange("(d o) -> d o", o=1).unsqueeze(0).to_broadcast([H, DH, 1])).then_inc(s_const, 16)
                e.dma_start(bias_o[:, :], t["bo"].rearrange("(o n) -> o n", o=1)).then_inc(s_const, 16)
                e.wait_ge(s_setup, n_setup)
                e.dma_start(t["x_sorted"].rearrange("(m p) d -> p m d", p=P),
                            zero[:, :].unsqueeze(1).to_broadcast([P, MT, D])).then_inc(s_pad, 16)
            windows(Steps(None), eng, sp_body, setup)
            finish_sync(eng)


        @block.tensor
        def _(eng):
            def setup(e):
                e.wait_ge(s_const, n_const)
                e.wait_ge(s_setup, n_setup)
            windows(pe, eng, pe_body, setup)
            finish_pe(eng)

        @block.scalar
        def _(eng):
            def setup(e):
                e.wait_ge(s_const, n_const)
                e.wait_ge(s_setup, n_setup)
                nc.scalar.preload_act_table_set("natural_log_exp_and_others")
                nc.scalar.activation(neg_a[:, :], neg_a[:, :], ACT.Exp).then_inc(s_zero, 1)
                e.wait_ge(s_zero, 1)
                nc.scalar.mul(neg_a[:, :], neg_a[:, :], -1.0).then_inc(s_zero, 1)
                e.wait_ge(s_zero, 2)
            windows(act, eng, act_body, setup)
            finish_act(eng)

        @block.gpsimd
        def _(eng):
            def setup(e):
                e.wait_ge(s_setup, n_setup)
            windows(pool, eng, pool_body, setup)
            finish_pool(eng)

        @block.vector
        def _(eng):
            def setup(e):
                nc.vector.memset(S[0][:, :, :], 0.0).then_inc(s_setup, 1)
                for n in range(2):
                    nc.vector.memset(to_end[n][:, C - 1, :], 1.0).then_inc(s_setup, 1)
                nc.vector.memset(zero[:, :], 0.0).then_inc(s_setup, 1)
                nc.vector.memset(rms_eps[:, :], RMS_EPS).then_inc(s_setup, 1)
                e.wait_ge(s_const, n_const)
                nc.vector.memset(ln_eps[:, :], LN_EPS).then_inc(s_setup, 1)
                for row, src in ((w_proj[:, 5, :], w_a[:, :]), (dt_row[:, :], dt_in[:, :])):
                    nc.vector.tensor_scalar(row.rearrange("p (h d) -> p h d", d=DH),
                                            src.unsqueeze(2).to_broadcast([src.shape[0], H, DH]), -1.0, None,
                                            ALU.mult).then_inc(s_setup, 1)
                e.wait_ge(s_setup, n_setup)
            windows(dve, eng, dve_body, setup)
            finish_dve(eng)


def kernel(**inputs):
    import numpy as _np
    import concourse.bacc as _bacc
    from concourse import mybir as _mybir
    from concourse.bass_utils import run_bass_kernel_spmd as _run

    a = {k: _np.ascontiguousarray(v) for k, v in inputs.items()}
    f = _np.float32
    x = a["L0_attn_x"]
    chan = _np.arange(P)
    same_head = (chan[:, None] // DH == chan[None, :] // DH).astype(f)
    down = _np.zeros((E, IC * P, D), a["L0_ffn_down_w"].dtype)
    down[:, :I, :] = a["L0_ffn_down_w"].transpose(0, 2, 1)
    arrays = {
        "x_ct": x.reshape(NB, NW, T, D).transpose(3, 1, 0, 2).reshape(D, NW, WN),
        "x_tc": x.reshape(TW, NB // TW, NW, T, D).transpose(2, 1, 3, 0, 4).reshape(NW, P, TW * D),
        "w_q": a["L0_attn_Wq"].T, "w_k": a["L0_attn_Wk"].T, "w_v": a["L0_attn_Wv"].T,
        "w_g": a["L0_attn_Wg"].T, "w_b": a["L0_attn_Wb"].T, "w_a": a["L0_attn_Wa"].T,
        "w_o": a["L0_attn_Wo"].T, "w_r": a["L0_ffn_router_w"].T,
        "dt_bias": a["L0_attn_dt_bias"], "A_log": a["L0_attn_A_log"], "norm_w": a["L0_attn_norm_w"],
        "bo": a["L0_attn_bo"],
        "gate_w": a["L0_ffn_gate_w"].transpose(2, 0, 1), "up_w": a["L0_ffn_up_w"].transpose(2, 0, 1),
        "down_w": down.reshape(E, IC, P, D).transpose(2, 1, 0, 3),
        "ident": _np.eye(P, dtype=f), "heads": same_head, "heads_q": same_head * f(DH), "heads_mean": same_head / f(DH),
        "below": (chan[:, None] < chan[None, :]).astype(f), "ones": _np.ones((P, P), f),
        "iota_e": _np.tile(_np.arange(E, dtype=f), (P, 1)), "iota_t": _np.arange(MT, dtype=f)[None, :],
    }
    arrays = {k: _np.ascontiguousarray(v) for k, v in arrays.items()}
    nc = _bacc.Bacc("TRN2", target_bir_lowering=False, num_devices=1)
    dram = {k: nc.dram_tensor(f"in_{k}", v.shape, _mybir.dt.from_np(v.dtype), kind="ExternalInput").ap()
            for k, v in arrays.items()}
    names = ("w_q", "w_k", "w_v", "w_g", "w_b", "w_a", "w_o", "w_r", "ident", "heads", "heads_q", "heads_mean", "below", "ones",
             "iota_e", "iota_t")
    dram["consts"] = {k: dram[k] for k in names}
    dram["k_dram"] = [nc.dram_tensor(f"k_dram{n}", (P, WN), F32, kind="Internal").ap() for n in range(2)]
    dram["q_dram"] = [nc.dram_tensor(f"q_dram{n}", (P, WN), F32, kind="Internal").ap() for n in range(2)]
    dram["x_sorted"] = nc.dram_tensor("x_sorted", (MT * P, D), F32, kind="Internal").ap()
    dram["y_sorted"] = nc.dram_tensor("y_sorted", (MT * P, D), F32, kind="Internal").ap()
    dram["out"] = nc.dram_tensor("out_0", (NW, P, TW * D), F32, kind="ExternalOutput").ap()
    block_kernel(nc, dram)
    r = _run(nc, [{f"in_{k}": v for k, v in arrays.items()}], core_ids=[0])
    y = r.results[0]["out_0"].reshape(NW, NB // TW, T, TW, D)
    return _np.ascontiguousarray(y.transpose(3, 1, 0, 2, 4).reshape(NB, L, D))
```

```python
from contextlib import ExitStack

import concourse.bass as bass
from concourse import mybir

F32 = mybir.dt.float32
I32 = mybir.dt.int32
ALU = mybir.AluOpType
ACT = mybir.ActivationFunctionType
AX = mybir.AxisListType.X

P = 128
NB, L, D = 16, 512, 128
H, DH = 16, 8
T, C = 32, 4
NW, NCH = L // T, T // C
WN = NB * T
NN = NB * NCH
TW = WN // P
NT = NW * TW
E, I = 8, 352
IC = (I + P - 1) // P
MT = NT + E
NT_A = NT - 2 * TW
REGION = NT * P + P
NS = 4
LN_EPS, RMS_EPS = 1e-5, 1e-6

PRE_ONLY, FIRST, FULL, LAST, POST_ONLY = range(5)
HAS_PRE = (True, True, True, False, False)
HAS_CHAIN = (False, True, True, True, False)
HAS_POST = (False, False, True, True, True)


class Win:

    def __init__(self, i, par):
        self.i, self.par = i, par

    @property
    def w(self):
        return self.i * 2 + self.par

    def shift(self, n):
        return Win(self.i + (self.par + n) // 2, (self.par + n) % 2)


class Steps:

    def __init__(self, sem):
        self.sem, self.order = sem, {}

    def count(self, kind):
        return len(self.order[kind])

    def value(self, label, kind, body):
        at = self.order[kind].index(label) + 1
        if kind == PRE_ONLY:
            return at
        at = at + self.count(PRE_ONLY)
        if kind == FIRST:
            return at
        at = at + self.count(FIRST)
        if kind == POST_ONLY:
            return at + (NW - 2) * self.count(FULL) + self.count(LAST)
        return (body - 1) * self.count(FULL) + at


def block_kernel(nc, t):
    ctx = ExitStack()
    with ctx:
        def sb(name, shape, dt=F32):
            return ctx.enter_context(nc.sbuf_tensor(name, shape, dt))

        def sem(name):
            return ctx.enter_context(nc.semaphore(name))

        def two(name, shape):
            return [sb(f"{name}{n}", shape) for n in range(2)]

        w_proj = sb("w_proj", [P, 6, D])
        w_a = sb("w_a", [P, H])
        w_o = sb("w_o", [P, D])
        w_r = sb("w_r", [P, E])
        ident = sb("ident", [P, P])
        heads = sb("heads", [P, P])
        heads_q = sb("heads_q", [P, P])
        heads_mean = sb("heads_mean", [P, P])
        below = sb("below", [P, P])
        ones = sb("ones", [P, P])
        bias_o = sb("bias_o", [1, D])
        iota_e = sb("iota_e", [P, E])
        neg_a = sb("neg_a", [P, 1])
        norm_w = sb("norm_w", [P, 1])
        dt_row = sb("dt_row", [1, P])
        dt_in = sb("dt_in", [1, H])
        rms_eps = sb("rms_eps", [P, 1])
        ln_eps = sb("ln_eps", [P, 1])
        no_token = sb("no_token", [P, D + 1])
        x1_all = sb("x1_all", [P, NT, D + 1])
        logits = sb("logits", [P, NT, E])
        token = logits[:, :, :].rearrange("p t e -> p (t e)")[:, 0:NT]
        stats = sb("stats", [P, TW, 6])
        mv = sb("mv", [P, TW, 2])
        rstd = sb("rstd", [P, TW])
        shift = sb("shift", [P, TW])
        settle = sb("settle", [P, 1])
        place = sb("place", [P, NT], I32)
        start_at = [sb(f"start_at{n}", [P, E]) for n in range(3)]

        att = ExitStack()
        att.__enter__()

        def sa(name, shape):
            return att.enter_context(nc.sbuf_tensor(name, shape, F32))

        def two_a(name, shape):
            return [sa(f"{name}{n}", shape) for n in range(2)]

        x_ct = two_a("x_ct", [P, WN])
        x_tc = sa("x_tc", [P, TW * D])
        k_rep = two_a("k_rep", [P, DH, WN])
        q_rep = two_a("q_rep", [P, DH, WN])
        beta_v = two_a("beta_v", [P, WN])
        beta_gam = two_a("beta_gam", [P, WN])
        gam = two_a("gam", [P, WN])
        to_end = two_a("to_end", [P, C, NN])
        akk = two_a("akk", [P, 9, NN])
        aqk = two_a("aqk", [P, 10, NN])
        delta = two_a("delta", [P, C, NN])
        gate_in = sa("gate_in", [P, WN])
        gate = two_a("gate", [P, WN])
        zbg_r = sa("zbg_r", [P, 3, WN])
        zbg_a = sa("zbg_a", [P, 3, WN])
        alpha, beta, g_sig = (zbg_a[:, n, :] for n in range(3))
        spare = zbg_r[:, :, :].rearrange("p a (b n) -> p (a b) n", n=NN)
        kk, beta_near, beta_far = spare[:, 0:6, :], spare[:, 6:9, :], spare[:, 9:12, :]
        kq_s, kq_sq = sa("kq_s", [P, 2, WN]), sa("kq_sq", [P, 2, WN])
        k_s, q_s, q_scaled = kq_s[:, 0, :], kq_s[:, 1, :], kq_sq[:, 1, :]
        far = sa("far", [P, 3, NN])
        qk = sa("qk", [P, 10, NN])
        S = [sa(f"S{n}", [P, NB, DH]) for n in range(NS)]
        ks = sa("ks", [P, C, NB])
        tri = sa("tri", [P, C - 1, NB])
        d_end = sa("d_end", [P, C, NB])
        upd = sa("upd", [P, NB, DH, C + 1])
        q_prod = [sa(f"q_prod{n}", [P, DH, 2, C, NB]) for n in range(3)]
        q_prod = [q_prod[n] for n in (0, 1, 2, 1)]
        y_prod = qk
        y_sq = sa("y_sq", [P, WN])
        ctx_t = sa("ctx_t", [P, WN])
        x1 = sa("x1", [P, TW, D])
        y_n = x1[:, :, :].rearrange("p i n -> p (i n)")
        x1_ct = y_sq[:, :].rearrange("p (i n) -> p i n", i=TW)

        psum = ctx.enter_context(nc.psum_tensor("banks", [P, 8, WN], F32))
        pb = [psum[:, n, :] for n in range(8)]
        zbg_ps, kq_ps = psum[:, 0:3, :], psum[:, 3:5, :]
        y_ps, post_ps = pb[5:7], pb[7]

        s_const, s_setup, s_neg_a = sem("s_const"), sem("s_setup"), sem("s_neg_a")
        s_xct = [sem(f"s_xct{n}") for n in range(2)]
        s_xtc = [sem(f"s_xtc{n}") for n in range(2)]
        s_kout, s_qout = sem("s_kout"), sem("s_qout")
        s_krep, s_qrep = ([sem(f"s_{n}rep{m}") for m in range(2)] for n in "kq")
        act, dve, pool, pe = (Steps(sem(f"s_{n}")) for n in ("act", "dve", "pool", "pe"))

        att.close()
        U = 8
        NG = MT // U
        gate_up_we = sb("gate_up_we", [P, E, 2, I])
        down_we = sb("down_we", [P, IC, E, D])
        tiles_i = sb("tiles_i", [P, E], I32)
        tiles_f = sb("tiles_f", [P, E])
        tile_end = sb("tile_end", [P, E])
        route_b = sb("route_b", [P, 4 * (NT - NT_A) * E + 2 * NT])
        iota_t = sb("iota_t", [1, MT])
        past = sb("past", [1, MT, E])
        row_at_f, row_at = sb("row_at_f", [1, MT]), sb("row_at", [1, MT], I32)
        fill_at = sb("fill_at", [1, E], I32)
        coef = sb("coef", [1, E])
        expert_f = sb("expert_f", [1, MT])
        expert_at = sb("expert_at", [1, MT], I32)
        xs = [sb(f"xs{n}", [P, D + 1]) for n in range(U)]
        NX = 4
        xs_t = [sb(f"xs_t{n}", [P, P]) for n in range(NX)]
        w_tile = [sb(f"w_tile{n}", [P, 2, IC * P]) for n in range(NX)]
        silu = two("silu", [P, IC * P])
        hid = two("hid", [P, IC * P])
        res2 = [sb(f"res2_{n}", [P, D]) for n in range(U)]
        res2_old = [sb(f"res2_old{n}", [P, D]) for n in range(U)]
        stats2 = sb("stats2", [P, 6])
        mv2, mv2_old = sb("mv2", [P, U, 2]), sb("mv2_old", [P, U, 2])
        row_f, row_old = sb("row_f", [P, U]), sb("row_old", [P, U], I32)
        rstd2 = sb("rstd2", [P, U])
        pool_settle = sb("pool_settle", [P, 1])
        rows_out = [sb(f"rows_out{n}", [P, D]) for n in range(U)]

        s_iota, s_wexp = sem("s_iota"), sem("s_wexp")
        s_route, s_count, s_pad = sem("s_route"), sem("s_count"), sem("s_pad")
        s_sorted = sem("s_sorted")
        s_w = [sem(f"s_w{n}") for n in range(NX)]
        s_xs, s_scat = ([sem(f"s_{m}{n}") for n in range(U)] for m in ("xs", "scat"))
        s_xturn, s_xt, s_gate, s_up, s_silu, s_hid, s_down, s_sum, s_stat, s_row, s_hand, s_rstd, s_norm = (
            sem(f"s_{n}") for n in ("xturn", "xt", "gate", "up", "silu", "hid", "down", "sum", "stat", "row", "hand",
                                    "rstd2", "norm"))
        s_kept, s_settle, s_var, s_fill = sem("s_kept"), sem("s_settle"), sem("s_var"), sem("s_fill")
        turn_ps, down_ps, g_ps, u_ps = (pb[0], pb[7]), pb[1:3], pb[3:5], pb[5:7]

        def attention_done(eng):
            for st, last in ((pe, "router"), (act, "logits"), (pool, "ctx"), (dve, "ln_shift")):
                eng.wait_ge(st.sem, st.value(last, POST_ONLY, NW))

        def route_buffers(mem, n_tiles):
            n = n_tiles * E
            b = [mem[:, k * n:(k + 1) * n].rearrange("p (t e) -> p t e", e=E) for k in range(4)]
            return b + [mem[:, 4 * n + k * n_tiles:4 * n + (k + 1) * n_tiles] for k in range(2)]

        parts = ((0, NT_A, route_buffers(k_rep[0][:, :, :].rearrange("p d n -> p (d n)"), NT_A)),
                 (NT_A, NT, route_buffers(route_b[:, :], NT - NT_A)))

        class Route:

            def __init__(self, eng):
                self.eng, self.n = eng, 0

            def link(self, ins):
                self.n += 1
                ins.then_inc(s_route, 1)
                self.eng.wait_ge(s_route, self.n)

            def part(self, k):
                v, link = nc.vector, self.link
                t0, t1, (cand, one_hot, total, before, top, place_f) = parts[k]
                n = t1 - t0

                def over_t(x):
                    return x.unsqueeze(2).to_broadcast([P, n, E])

                def over_e(x):
                    return x.unsqueeze(1).to_broadcast([P, n, E])
                if k == 0:
                    link(v.tensor_scalar(start_at[0][:, :], iota_e[:, :], float(REGION), None, ALU.mult))
                part_logits = logits[:, t0:t1, :]
                link(v.tensor_reduce(top, part_logits, AX, ALU.max))
                link(v.tensor_tensor(cand, part_logits, over_t(top), ALU.is_equal))
                link(v.scalar_tensor_tensor(cand, cand, -float(E), over_e(iota_e[:, :]), ALU.mult, ALU.add))
                link(v.tensor_reduce(top, cand, AX, ALU.min))
                link(v.tensor_tensor(one_hot, cand, over_t(top), ALU.is_equal))
                assert self.n == n_route_hot[k]
                self.eng.wait_ge(s_count, 2 * k + 2)
                link(v.tensor_copy(total.rearrange("p t e -> p (t e)"), pb[1][:, 0:n * E]))
                for e in range(E):
                    link(v.tensor_tensor_scan(before[:, :, e], ones[:, 0:n], total[:, :, e], 0.0, ALU.mult, ALU.add))
                link(v.tensor_tensor(start_at[k + 1][:, :], before[:, n - 1, :], start_at[k][:, :], ALU.add))
                link(v.tensor_tensor(before, before, total, ALU.subtract))
                link(v.tensor_tensor(before, before, over_e(start_at[k][:, :]), ALU.add))
                link(v.tensor_tensor(before, pb[0][:, 0:n * E].rearrange("p (t e) -> p t e", e=E), before, ALU.add))
                link(v.tensor_tensor(before, before, one_hot, ALU.mult))
                link(v.tensor_reduce(place_f, before, AX, ALU.add))
                link(v.tensor_copy(place[:, t0:t1], place_f))
                assert self.n == n_placed[k]

            def tiles(self):
                v, link = nc.vector, self.link
                link(v.tensor_copy(fill_at[:, :], start_at[2][0:1, :]))
                assert self.n == n_filled
                link(v.tensor_tensor(tiles_f[:, :], start_at[2][:, :], start_at[0][:, :], ALU.subtract))
                link(v.tensor_scalar(tiles_f[:, :], tiles_f[:, :], float(P - 1), None, ALU.add))
                link(v.tensor_copy(tiles_i[:, :], tiles_f[:, :]))
                link(v.tensor_scalar(tiles_i[:, :], tiles_i[:, :], P.bit_length() - 1, None, ALU.logical_shift_right))
                link(v.tensor_copy(tiles_f[:, :], tiles_i[:, :]))
                link(v.tensor_tensor_scan(tile_end[:, :], ones[:, 0:E], tiles_f[:, :], 0.0, ALU.mult, ALU.add))
                link(v.tensor_tensor(past[:, :, :], tile_end[0:1, :].unsqueeze(1).to_broadcast([1, MT, E]),
                                     iota_t[:, :].unsqueeze(2).to_broadcast([1, MT, E]), ALU.is_le))
                link(v.tensor_reduce(expert_f[:, :], past[:, :, :], AX, ALU.add))
                link(v.tensor_scalar(expert_f[:, :], expert_f[:, :], float(E - 1), None, ALU.min))
                link(v.tensor_copy(expert_at[:, :], expert_f[:, :]))
                link(v.tensor_scalar(coef[:, :], tiles_f[0:1, :], -float(P), float(REGION), ALU.mult, ALU.add))
                link(v.tensor_tensor(past[:, :, :], past[:, :, :], coef[:, :].unsqueeze(1).to_broadcast([1, MT, E]),
                                     ALU.mult))
                link(v.tensor_reduce(row_at_f[:, :], past[:, :, :], AX, ALU.add))
                link(v.scalar_tensor_tensor(row_at_f[:, :], iota_t[:, :], float(P), row_at_f[:, :], ALU.mult, ALU.add))
                link(v.tensor_copy(row_at[:, :], row_at_f[:, :]))
                assert self.n == n_route_all

        n_part = 13 + E
        n_route_hot = (6, 1 + n_part + 5)
        n_placed = (1 + n_part, 1 + 2 * n_part)
        n_filled = n_placed[1] + 1
        n_route_all = n_filled + 15

        def count(eng, k):
            t0, t1, (_, one_hot, *_) = parts[k]
            hot = one_hot.rearrange("p t e -> p (t e)")
            eng.wait_ge(s_route, n_route_hot[k])
            for ps, by in ((pb[0], below), (pb[1], ones)):
                nc.tensor.matmul(ps[:, 0:(t1 - t0) * E], by[:, :], hot, start=True, stop=True).then_inc(s_count, 1)

        def to_sorted(eng, t0, t1):
            for m in range(t0, t1):
                eng.indirect_dma_start(t["x_sorted"], bass.IndirectOffsetOnAxis(ap=place[:, m:m + 1], axis=0),
                                       x1_all[:, m, :], None).then_inc(s_sorted, 16)

        def before_last(eng):
            if eng is nc.tensor:
                eng.wait_ge(dve.sem, dve.value("aqk_far", FULL, NW - 2))
                eng.wait_ge(act.sem, act.value("aqk_same", FULL, NW - 2))
                count(eng, 0)
            if eng is nc.vector:
                eng.wait_ge(act.sem, act.value("logits", FULL, NW - 2))
                for h in range(2):
                    eng.wait_ge(s_link["S", h], (NW - 1) * NCH)
                routing.part(0)
            if eng is nc.gpsimd:
                eng.wait_ge(s_pad, 16)

        def all_groups(eng, body):
            body(0)
            body(1)
            with eng.Fori(2, NG - 1) as i:
                body(i)
            body(NG - 1)

        def at_least(eng, s, value):
            if not isinstance(value, int) or value > 0:
                eng.wait_ge(s, value)

        def there(tile):
            return not isinstance(tile, int) or tile < MT

        def finish_sync(eng):
            attention_done(eng)
            eng.dma_start(iota_t[:, :], t["iota_t"]).then_inc(s_iota, 16)
            eng.dma_start(gate_up_we[:, :, 0, :], t["gate_w"]).then_inc(s_wexp, 16)
            eng.dma_start(gate_up_we[:, :, 1, :], t["up_w"]).then_inc(s_wexp, 16)
            eng.dma_start(down_we[:, :, :, :], t["down_w"]).then_inc(s_wexp, 16)
            eng.wait_ge(s_route, n_filled)
            fills = [eng.value_load(fill_at[0:1, e:e + 1], min_val=0, max_val=E * REGION - P) for e in range(E)]
            eng.wait_ge(s_route, n_route_all)

            def weights(i, u):
                i, u = i + u // U, u % U
                tile = i * U + u
                if there(tile):
                    at = eng.value_load(expert_at[0:1, bass.ds(tile, 1)], min_val=0, max_val=E - 1) * (2 * I)
                    at_least(eng, s_up, tile - NX + 1)
                    eng.dma_start(w_tile[u % NX][:, :, 0:I],
                                  gate_up_we[:, :, :, :].rearrange("p e g i -> p (e g i)")[:, bass.ds(at, 2 * I)]
                                  .rearrange("p (g i) -> p g i", g=2)).then_inc(s_w[u % NX], 16)
            eng.wait_ge(s_wexp, 48)
            eng.wait_ge(s_fill, NX)
            for u in range(NX):
                weights(0, u)
            eng.wait_ge(s_sorted, 16 * NT)
            for row in fills:
                eng.dma_start(t["x_sorted"][bass.ds(row, P), :], no_token[:, :]).then_inc(s_pad, 16)

            def group(i):
                for u in range(U):
                    weights(i, u + NX)
            all_groups(eng, group)
            for u in range(U):
                eng.wait_ge(s_scat[u], 16 * NG)

        def finish_pe(eng):
            attention_done(eng)
            mm, tr = nc.tensor.matmul, nc.tensor.transpose
            count(eng, 1)
            eng.wait_ge(s_route, n_route_all)
            eng.wait_ge(s_wexp, 48)

            def x_turn(i, u):
                i, u = i + u // U, u % U
                tile = i * U + u
                if there(tile):
                    eng.wait_ge(s_xs[u], (i + 1) * 16)
                    at_least(eng, s_xt, tile - 1)
                    tr(turn_ps[u % 2][:, 0:P], xs[u][:, 0:D], ident[:, :]).then_inc(s_xturn, 1)

            def gate_up(i, u):
                i, u = i + u // U, u % U
                tile, par = i * U + u, u % 2
                if there(tile):
                    eng.wait_ge(s_xt, tile + 1)
                    at_least(eng, s_hid, tile - 1)
                    eng.wait_ge(s_w[u % NX], (i * (U // NX) + u // NX + 1) * 16)
                    for g, ps in enumerate((g_ps, u_ps)):
                        for c in range(IC):
                            piece = slice(c * P, (c + 1) * P)
                            last = mm(ps[par][:, piece], w_tile[u % NX][:, g, piece], xs_t[u % NX][:, :],
                                      start=True, stop=True)
                        last.then_inc(s_gate if g == 0 else s_up, 1)

            def down(i, u):
                tile, par = i * U + u, u % 2
                at = eng.value_load(expert_at[0:1, bass.ds(tile, 1)], min_val=0, max_val=E - 1) * D
                eng.wait_ge(s_hid, tile + 1)
                at_least(eng, s_sum, tile - 1)
                for c in range(IC):
                    last = mm(down_ps[par][:, 0:D], hid[par][:, c * P:(c + 1) * P],
                              down_we[:, c, :, :].rearrange("p e d -> p (e d)")[:, bass.ds(at, D)],
                              start=(c == 0), stop=(c == IC - 1))
                last.then_inc(s_down, 1)

            def group(i):
                for u in range(U):
                    x_turn(i, u + 3)
                    gate_up(i, u + 2)
                    down(i, u)
            for u in range(3):
                x_turn(0, u)
            for u in range(2):
                gate_up(0, u)
            all_groups(eng, group)

        def finish_act(eng):
            attention_done(eng)
            A = nc.scalar.activation
            eng.wait_ge(s_route, n_route_all)

            def row_of(tile):
                return eng.value_load(row_at[0:1, bass.ds(tile, 1)], min_val=0, max_val=E * REGION + (E - 1) * P)

            def load(i, u):
                i, u = i + u // U, u % U
                tile = i * U + u
                if there(tile) and not (isinstance(tile, int) and tile < U):
                    row = row_of(tile)
                    eng.wait_ge(s_row, tile - U + 1)
                    eng.dma_start(xs[u][:, :], t["x_sorted"][bass.ds(row, P), :]).then_inc(s_xs[u], 16)
            rows = [row_of(u) for u in range(U)]
            eng.wait_ge(s_pad, 16 * (1 + E))
            for u in range(U):
                eng.dma_start(xs[u][:, :], t["x_sorted"][bass.ds(rows[u], P), :]).then_inc(s_xs[u], 16)

            def x_copy(i, u):
                i, u = i + u // U, u % U
                tile, par = i * U + u, u % 2
                if there(tile):
                    eng.wait_ge(s_xturn, tile + 1)
                    at_least(eng, s_up, tile - NX + 1)
                    A(xs_t[u % NX][:, :], turn_ps[par][:, 0:P], ACT.Copy).then_inc(s_xt, 1)

            def silu_of(i, u):
                i, u = i + u // U, u % U
                tile, par = i * U + u, u % 2
                if there(tile):
                    eng.wait_ge(s_gate, tile + 1)
                    at_least(eng, s_hid, tile - 1)
                    A(silu[par][:, :], g_ps[par][:, 0:IC * P], ACT.Silu).then_inc(s_silu, 1)

            def rstd_of(i):
                nc.scalar.preload_act_table_set("natural_log_exp_and_others")
                eng.wait_ge(s_hand, 2 * (i + 1))
                A(rstd2[:, :], mv2_old[:, :, 1], ACT.Ln, bias=ln_eps[:, 0:1]).then_inc(s_rstd, 1)
                eng.wait_ge(s_rstd, 2 * i + 1)
                A(rstd2[:, :], rstd2[:, :], ACT.Exp, scale=-0.5).then_inc(s_rstd, 1)
                nc.scalar.preload_act_table_set("silu_and_others")

            def group(i):
                for u in range(U):
                    x_copy(i, u + 3)
                    silu_of(i, u + 1)
                    load(i, u - 1 + U)
                    if u == 0 and not (isinstance(i, int) and i == 0):
                        rstd_of(i - 1)
            for u in range(3):
                x_copy(0, u)
            silu_of(0, 0)
            all_groups(eng, group)
            rstd_of(NG - 1)

        def finish_pool(eng):
            attention_done(eng)
            eng.wait_ge(s_route, n_placed[1])
            to_sorted(eng, NT_A, NT)

            past_end = eng.to_reg(NT * P - 1)

            def scatter(i, u):
                eng.indirect_dma_start(t["out"], bass.IndirectOffsetOnAxis(ap=row_old[:, u:u + 1], axis=0),
                                       rows_out[u][:, :], None, bounds_check=past_end, oob_is_err=False) \
                    .then_inc(s_scat[u], 16)

            def group(i):
                for u in range(U):
                    if 2 <= u < 2 + U // 2 and not (isinstance(i, int) and i == 0):
                        eng.wait_ge(s_norm, (i - 1) * U + 2 * (u - 2) + 2)
                        at_least(eng, s_settle, (i - 1) * (U // 2) + u - 2)
                        nc.gpsimd.tensor_tensor(pool_settle[:, :], ones[:, 0:1], ones[:, 0:1], ALU.mult) \
                            .then_inc(s_settle, 1)
                        scatter(i - 1, 2 * (u - 2))
                        scatter(i - 1, 2 * (u - 2) + 1)
                    eng.wait_ge(s_sum, i * U + u + 1)
                    at_least(eng, s_norm, (i - 1) * U + u + 1)
                    nc.gpsimd.tensor_tensor(res2_old[u][:, :], res2[u][:, :], ones[:, :], ALU.mult).then_inc(s_kept, 1)
            all_groups(eng, group)
            for u in range(U):
                eng.wait_ge(s_norm, (NG - 1) * U + u + 1)
                scatter(NG - 1, u)

        def finish_dve(eng):
            attention_done(eng)
            v = nc.vector
            routing.part(1)
            eng.wait_ge(s_iota, 16)
            routing.tiles()
            for n in range(NX):
                v.memset(w_tile[n][:, :, I:IC * P], 0.0).then_inc(s_fill, 1)

            def hidden(i, u):
                i, u = i + u // U, u % U
                tile, par = i * U + u, u % 2
                if there(tile):
                    eng.wait_ge(s_silu, tile + 1)
                    eng.wait_ge(s_up, tile + 1)
                    at_least(eng, s_down, tile - 1)
                    v.tensor_tensor(hid[par][:, :], u_ps[par][:, 0:IC * P], silu[par][:, :], ALU.mult).then_inc(s_hid, 1)

            def row_sum(i, u):
                tile, par = i * U + u, u % 2
                eng.wait_ge(s_down, tile + 1)
                at_least(eng, s_kept, (i - 1) * U + u + 1)
                v.tensor_tensor(res2[u][:, :], down_ps[par][:, 0:D],
                                xs[u][:, 0:D], ALU.add).then_inc(s_sum, 1)
                at_least(eng, s_hand, 2 * i)
                v.tensor_copy(row_f[:, u:u + 1], xs[u][:, D:D + 1]).then_inc(s_row, 1)
                eng.wait_ge(s_sum, tile + 1)
                at_least(eng, s_var, tile)
                v.bn_stats(stats2[:, :], res2[u][:, :]).then_inc(s_stat, 1)

            def row_var(i, u):
                tile = i * U + u
                eng.wait_ge(s_stat, tile + 1)
                v.tensor_copy(settle[:, :], ones[:, 0:1])
                v.bn_aggr(mv2[:, u, :], stats2[:, :]).then_inc(s_var, 1)

            def hand_over(i):
                eng.wait_ge(s_var, (i + 1) * U)
                at_least(eng, s_norm, i * U)
                v.tensor_copy(mv2_old[:, :, :], mv2[:, :, :]).then_inc(s_hand, 1)
                eng.wait_ge(s_row, (i + 1) * U)
                for u in range(U):
                    at_least(eng, s_scat[u], 16 * i)
                v.tensor_copy(row_old[:, :], row_f[:, :]).then_inc(s_hand, 1)

            def norm(i, u):
                eng.wait_ge(s_rstd, 2 * (i + 1))
                eng.wait_ge(s_hand, 2 * (i + 1))
                eng.wait_ge(s_kept, i * U + u + 1)
                v.tensor_scalar(rows_out[u][:, :], res2_old[u][:, :],
                                mv2_old[:, u, 0:1], rstd2[:, u:u + 1], ALU.subtract, ALU.mult).then_inc(s_norm, 1)

            def group(i):
                later = not (isinstance(i, int) and i == 0)
                if later:
                    hand_over(i - 1)
                for u in range(U):
                    hidden(i, u + 1)
                    row_sum(i, u)
                    if later and 1 <= u < 1 + U // 2:
                        norm(i - 1, 2 * (u - 1))
                    row_var(i, u)
                    if later and 1 <= u < 1 + U // 2:
                        norm(i - 1, 2 * (u - 1) + 1)
            hidden(0, 0)
            all_groups(eng, group)
            hand_over(NG - 1)
            for u in range(U):
                norm(NG - 1, u)

        block = ctx.enter_context(nc.Block())

        def slots(tile):
            return tile.rearrange("p (n j) -> p j n", j=C)

        def chunk_jb(tile, c):
            return tile.rearrange("p (b c j) -> p c j b", c=NCH, j=C)[:, c, :, :]

        def slot_chunk(tile, c):
            return tile[:, :, :].rearrange("p s (b c) -> p c s b", c=NCH)[:, c, :, :]

        def rep_chunk(tile, c, order):
            return tile[:, :, :].rearrange("p d (b c j) -> p c d b j", c=NCH, j=C)[:, c, :, :, :] \
                .rearrange(f"p d b j -> p {order}")

        links = ["k_prod", "k_sum", "decay", "k_gam", "rhs"]
        links += [f"{m}{j}" for j in range(C - 1) for m in ("tri", "sub")] + ["d_end", "upd", "S"]
        s_link = {(name, h): sem(f"s_{name}_{h}") for name in links for h in range(2)}
        routing = Route(nc.vector)

        class Body:

            def __init__(self, steps, eng, kind, win, dry):
                self.steps, self.eng, self.kind, self.win, self.dry = steps, eng, kind, win, dry
                if dry:
                    steps.order[kind] = []
                self.at = 0

            def step(self, label, ins):
                if self.dry:
                    self.steps.order[self.kind].append(label)
                else:
                    assert self.steps.order[self.kind][self.at] == label
                    ins().then_inc(self.steps.sem, 1)
                self.at += 1

            def wait(self, steps, label, back=0):
                if self.dry:
                    return
                kind, body = self.kind, self.win.w
                if back:
                    if not isinstance(body, int):
                        kind = FULL
                    else:
                        m = body - back
                        kind = PRE_ONLY if m == -1 else FIRST if m == 0 else LAST if m == NW - 1 else FULL
                        if m < -1:
                            return
                if label not in steps.order[kind]:
                    return
                self.eng.wait_ge(steps.sem, steps.value(label, kind, body - back))

            def link(self, name, c, back=0):
                w = self.win.w - back
                if self.dry or (isinstance(w, int) and not 0 <= w < NW):
                    return
                for h in range(2):
                    self.eng.wait_ge(s_link[name, h], w * NCH + c + 1)

            def own(self):
                if self.dry or not self.at:
                    return
                label = self.steps.order[self.kind][self.at - 1]
                self.eng.wait_ge(self.steps.sem, self.steps.value(label, self.kind, self.win.w))

            def dma(self, sems, win, per=16):
                if not self.dry:
                    self.eng.wait_ge(sems[win.par], (win.i + 1) * per)

            def dma1(self, s, win, per=16):
                if not self.dry:
                    self.eng.wait_ge(s, (win.w + 1) * per)

        def pe_body(b):
            w = b.win
            pre, chain, post = HAS_PRE[b.kind], HAS_CHAIN[b.kind], HAS_POST[b.kind]
            nxt, prv = w.shift(1), w.shift(-1)
            mm, tr = nc.tensor.matmul, nc.tensor.transpose

            def project(label, n, out, bias=False):
                def go():
                    if bias:
                        mm(out, dt_row[:, :], ones[0:1, :].unsqueeze(1).to_broadcast([1, TW, P]), start=True, stop=False)
                    return mm(out, w_proj[:, n, :], x_ct[nxt.par][:, :], start=not bias, stop=True)
                b.step(label, go)

            def head_sum(label, src, out, ready, by=heads):
                b.wait(*ready)
                b.step(label, lambda: mm(out[:, 0:src.shape[1]], by[:, :], src, start=True, stop=True))

            def y_chunks(m, win, back=0):
                b.wait(pool, f"q_prod{2 * m + 1}", back)
                if m == 0:
                    b.wait(act, "y_sq", back=1)
                    b.wait(dve, "y_n", back=1)
                out = y_ps[win.par].rearrange("p (j b c) -> p c j b", j=C, c=NCH)[:, 2 * m:2 * m + 2, :, :]

                def go():
                    for d in range(DH):
                        i = mm(out, ident[:, :], q_prod[m][:, d, :, :, :], start=(m == 0 and d == 0), stop=(d == DH - 1),
                               skip_group_check=True)
                    return i
                b.step(f"y{m}", go)

            def y_deltas():
                b.wait(pool, "y_prod3")
                y = y_ps[prv.par].rearrange("p (j n) -> p j n", j=C)

                def go():
                    at = 0
                    for d in range(C):
                        i = mm(y[:, d:C, :], ident[:, :], y_prod[:, at:at + C - d, :], start=False, stop=True,
                               skip_group_check=True)
                        at += C - d
                    return i
                b.step("y", go)

            def soft_sum(n, label):
                if n == 0:
                    b.wait(act, "zbg_ln")
                if n == 2:
                    b.wait(act, "gate_g")

                def go():
                    mm(zbg_ps[:, n, :], ident[:, :], zbg_r[:, n, :], start=True, stop=False)
                    return mm(zbg_ps[:, n, :], ident[:, :], zbg_a[:, n, :], start=False, stop=True)
                b.step(label, go)

            def y_mean():
                b.wait(act, "y_sq")
                b.wait(act, "logits", back=1)
                b.step("ms", lambda: mm(post_ps, heads_mean[:, :], y_sq[:, :], start=True, stop=True))

            def out_proj():
                if not b.dry:
                    b.dma(s_xtc, prv)
                b.wait(act, "rms")
                b.step("res", lambda: mm(post_ps, ident[:, :], x_tc[:, :], start=True, stop=False, skip_group_check=True))
                b.wait(pool, "ctx")

                def go():
                    mm(post_ps, ones[0:1, :], bias_o[0:1, :].unsqueeze(1).to_broadcast([1, TW, D]),
                       start=False, stop=False, skip_group_check=True)
                    for i in range(TW):
                        last = mm(post_ps[:, i * D:(i + 1) * D], ctx_t[:, i * P:(i + 1) * P], w_o[:, :],
                                  start=False, stop=True, skip_group_check=True)
                    return last
                b.step("attn", go)

            def turn():
                b.wait(act, f"x1_{TW - 1}")

                def go():
                    for i in range(TW):
                        last = tr(post_ps[:, i * P:(i + 1) * P], x1[:, i, :], ident[:, :])
                    return last
                b.step("turn", go)

            def router():
                b.wait(act, "x1_ct")

                def go():
                    for i in range(TW):
                        last = mm(post_ps[:, i * E:(i + 1) * E], x1_ct[:, i, :], w_r[:, :], start=True, stop=True)
                    return last
                b.step("router", go)

            qkf = qk[:, :, :].rearrange("p s n -> p (s n)")
            kkf = kk.rearrange("p s n -> p (s n)")
            if pre:
                if not b.dry:
                    b.dma(s_xct, nxt)
                b.wait(dve, "aqk_far", back=1)
                b.wait(act, "aqk_same", back=1)
                project("z", 5, zbg_ps[:, 0, :], True)
                project("b", 4, zbg_ps[:, 1, :])
                project("g", 3, zbg_ps[:, 2, :])
                b.wait(dve, "akk_far", back=1)
                project("k", 1, kq_ps[:, 0, :])
                project("q", 0, kq_ps[:, 1, :])
            if post:
                y_chunks(2, prv, back=1)
            if pre:
                b.wait(act, "kq_s")
                head_sum("nk", kq_sq[:, 0, :], kq_ps[:, 0, :], (act, "kq_sq"))
                head_sum("nq", kq_sq[:, 1, :], kq_ps[:, 1, :], (act, "kq_sq"), heads_q)
            if post:
                y_chunks(3, prv, back=1)
            if pre:
                soft_sum(0, "z_sum")
                soft_sum(1, "b_sum")
                soft_sum(2, "g_sum")
                b.wait(act, "alpha")
                project("v", 2, zbg_ps[:, 0, :])
            if post:
                y_deltas()
                y_mean()
            if chain:
                y_chunks(0, w)
            if post:
                out_proj()
            if chain:
                y_chunks(1, w)
            if pre:
                b.wait(act, "g_sig")
                b.wait(dve, "beta_v")
                head_sum("qk_same", qkf[:, 0:4 * NN], zbg_ps[:, 0, :], (pool, "qk_same"))
                head_sum("qk_near", qkf[:, 4 * NN:7 * NN], zbg_ps[:, 1, :], (pool, "qk_near"))
            if pre:
                head_sum("qk_far", qkf[:, 7 * NN:10 * NN], zbg_ps[:, 2, :], (pool, "qk_far2"))
            if pre:
                b.wait(act, "kq_ln")
                head_sum("kk_near", kkf[:, 0:3 * NN], kq_ps[:, 0, :], (pool, "kk_near"))
                head_sum("kk_far", kkf[:, 3 * NN:6 * NN], kq_ps[:, 1, :], (pool, "kk_far2"))
            if post:
                turn()
                router()

        def act_body(b):
            w = b.win
            pre, post = HAS_PRE[b.kind], HAS_POST[b.kind]
            nxt, prv = w.shift(1), w.shift(-1)
            A = nc.scalar.activation

            if pre:
                b.wait(pool, "beta_gam", back=1)
                b.wait(dve, "akk_far", back=1)
                b.wait(pe, "qk_far", back=1)
                b.wait(act, "to_end2", back=1)
                if not b.dry and not (isinstance(w.w, int) and w.w < 0):
                    b.dma1(s_kout, w)
                    b.dma1(s_qout, w)
                b.wait(pe, "g")
                b.step("zbg_relu", lambda: A(zbg_r[:, :, :], zbg_ps, ACT.Relu, scale=-1.0))
                b.step("zbg_abs", lambda: A(zbg_a[:, :, :], zbg_ps, ACT.Abs))
                b.wait(pe, "q")
                b.step("kq_sq", lambda: A(kq_sq[:, :, :], kq_ps, ACT.Square))
                b.step("kq_s", lambda: A(kq_s[:, :, :], kq_ps, ACT.Copy))
                b.wait(act, "zbg_abs")
                b.step("zbg_exp", lambda: A(zbg_a[:, :, :], zbg_a[:, :, :], ACT.Exp, scale=-1.0))
                b.own()
                b.step("zbg_ln", lambda: A(zbg_a[:, :, :], zbg_a[:, :, :], ACT.Ln, bias=1.0))
                b.wait(pe, "nq")
                b.step("kq_ln", lambda: A(kq_sq[:, :, :], kq_ps, ACT.Ln))
                b.own()
                b.step("kq_r", lambda: A(kq_sq[:, :, :], kq_sq[:, :, :], ACT.Exp, scale=-0.5))
                b.step("gate_g", lambda: A(gate_in[:, :], zbg_ps[:, 2, :], ACT.Copy, scale=norm_w[:, 0:1]))
            if pre:
                b.wait(pe, "z_sum")
                b.step("alpha", lambda: A(alpha, zbg_ps[:, 0, :], ACT.Exp, scale=neg_a[:, 0:1]))
                b.wait(pe, "b_sum")
                b.step("beta", lambda: A(beta, zbg_ps[:, 1, :], ACT.Exp, scale=-1.0))
                b.wait(pe, "g_sum")
                b.step("g_sig", lambda: A(g_sig, zbg_ps[:, 2, :], ACT.Exp, scale=-1.0))
                b.link("S", NCH - 1, back=1)
                b.wait(act, "alpha")
                b.step("gam0", lambda: A(slots(gam[nxt.par])[:, 0, :], slots(alpha)[:, 0, :], ACT.Copy))
                b.step("to_end2", lambda: A(to_end[nxt.par][:, 2, :], slots(alpha)[:, 3, :], ACT.Copy))
            if post:
                b.wait(pe, "y")
                b.wait(dve, "y_n", back=1)
                b.wait(pe, "router", back=1)
                b.step("y_sq", lambda: A(y_sq[:, :], y_ps[prv.par], ACT.Square))
                b.wait(pe, "ms")
                b.step("rms", lambda: A(y_sq[:, :], post_ps, ACT.Ln, bias=rms_eps[:, 0:1]))
                b.own()
                b.step("rms_r", lambda: A(y_sq[:, :], y_sq[:, :], ACT.Exp, scale=-0.5))
            if pre:
                b.wait(pool, "far2")
                b.step("to_end1", lambda: A(to_end[nxt.par][:, 1, :], far[:, 1, :], ACT.Copy))
                b.step("to_end0", lambda: A(to_end[nxt.par][:, 0, :], far[:, 2, :], ACT.Copy))
            if pre:
                b.wait(pe, "qk_same")
                b.step("aqk_same", lambda: A(aqk[nxt.par][:, 0:4, :].rearrange("p s n -> p (s n)"), zbg_ps[:, 0, :],
                                             ACT.Copy))
            if post:
                b.wait(dve, f"mv{TW - 1}")
                b.wait(act, f"x1_{TW - 1}", back=1)
                b.step("ln_ln", lambda: A(rstd[:, :], mv[:, :, 1], ACT.Ln, bias=ln_eps[:, 0:1]))
                b.own()
                b.step("ln_r", lambda: A(rstd[:, :], rstd[:, :], ACT.Exp, scale=-0.5))
                b.wait(dve, "ln_shift")
                b.wait(pool, "ctx")
                b.wait(pe, "turn", back=1)
                b.wait(act, "x1_keep", back=1)
                for i in range(TW):
                    b.step(f"x1_{i}", lambda: A(x1[:, i, :], post_ps[:, i * D:(i + 1) * D], ACT.Identity,
                                                bias=shift[:, i:i + 1], scale=rstd[:, i:i + 1]))
                b.wait(dve, "y_n")
                at = prv.w * TW
                b.own()
                b.step("x1_keep", lambda: A(x1_all[:, bass.ds(at, TW), 0:D], x1[:, :, :], ACT.Copy))
                b.wait(pe, "turn")
                b.step("x1_ct", lambda: A(x1_ct, post_ps.rearrange("p (i n) -> p i n", i=TW), ACT.Copy))
            if post:
                b.wait(pe, "router")
                b.step("logits", lambda: A(logits[:, bass.ds(at, TW), :],
                                           post_ps[:, 0:TW * E].rearrange("p (i e) -> p i e", i=TW), ACT.Copy))

        def pool_body(b):
            w = b.win
            pre, chain, post = HAS_PRE[b.kind], HAS_CHAIN[b.kind], HAS_POST[b.kind]
            nxt, prv = w.shift(1), w.shift(-1)
            tt = nc.gpsimd.tensor_tensor

            def mul(label, out, x, y, op=ALU.mult):
                b.step(label, lambda: tt(out, x, y, op))

            def q_times_s(c):
                if c == 0:
                    if not b.dry:
                        b.dma(s_qrep, w)
                    b.link("S", NCH - 1, back=1)
                else:
                    b.link("S", c - 1)
                if c % 2 == 0:
                    last, back = (("y0", 1), ("y3", 0), ("y2", 0), ("y1", 0))[c // 2]
                    b.wait(pe, last, back)
                s = S[c % NS][:, :, :].rearrange("p b d -> p d b").unsqueeze(2).to_broadcast([P, DH, C, NB])
                mul(f"q_prod{c}", q_prod[c // 2][:, :, c % 2, :, :], s, rep_chunk(q_rep[w.par], c, "d j b"))
                if b.kind == LAST and not b.dry:
                    if c == 0:
                        b.eng.wait_ge(s_route, n_placed[0])
                    to_sorted(b.eng, 3 * c, 3 * (c + 1))

            if post:
                b.link("sub2", NCH - 1, back=1)
                b.wait(pe, "qk_far", back=1)
                dl, aq, at = delta[prv.par], aqk[prv.par], 0
                for d in range(C):
                    mul(f"y_prod{d}", y_prod[:, at:at + C - d, :], aq[:, at:at + C - d, :], dl[:, 0:C - d, :])
                    at += C - d
            if chain:
                q_times_s(0)
                q_times_s(1)
            if pre:
                b.wait(act, "kq_r")
                mul("kq_n", kq_s[:, :, :], kq_s[:, :, :], kq_sq[:, :, :])
            if chain:
                q_times_s(2)
            if pre:
                al, bt = slots(alpha), slots(beta)
                gm = slots(gam[nxt.par])
                b.wait(act, "gam0")
                mul("far0", far[:, 0:2, :], al[:, 2:4, :], al[:, 1:3, :])
                mul("gam1", gm[:, 1, :], al[:, 0, :], al[:, 1, :])
                b.own()
                mul("far2", far[:, 2, :], far[:, 1, :], al[:, 1, :])
                mul("gam2", gm[:, 2, :], gm[:, 1, :], al[:, 2, :])
                b.own()
                mul("gam3", gm[:, 3, :], gm[:, 2, :], al[:, 3, :])
                b.own()
                mul("q_gam", q_scaled, q_s, gam[nxt.par][:, :])
                kn, qn = slots(k_s), slots(q_s)
                b.wait(pe, "y")
                mul("qk_same", qk[:, 0:4, :], qn, kn)
            if b.kind == POST_ONLY and not b.dry:
                to_sorted(b.eng, 3 * NCH, 3 * NCH + TW)
            if post:
                b.wait(dve, "y_n")
                b.wait(pe, "attn", back=1)
                mul("ctx", slots(ctx_t[:, :]), y_n.rearrange("p (j n) -> p j n", j=C), slots(gate[prv.par][:, :]))
            if pre:
                mul("qk_near", qk[:, 4:7, :], qn[:, 1:4, :], kn[:, 0:3, :])
                mul("qk_far", qk[:, 7:9, :], qn[:, 2:4, :], kn[:, 0:2, :])
                mul("qk_far2", qk[:, 9, :], qn[:, 3, :], kn[:, 0, :])
            if chain:
                q_times_s(3)
            if pre:
                b.wait(pe, "g_sum")
                mul("kk_near", kk[:, 0:3, :], kn[:, 1:4, :], kn[:, 0:3, :])
                mul("kk_far", kk[:, 3:5, :], kn[:, 2:4, :], kn[:, 0:2, :])
                mul("kk_far2", kk[:, 5, :], kn[:, 3, :], kn[:, 0, :])
                b.wait(act, "beta")
                mul("beta_near", beta_near, bt[:, 1:4, :], al[:, 1:4, :])
                mul("beta_far", beta_far[:, 0:2, :], bt[:, 2:4, :], far[:, 0:2, :])
                mul("beta_far2", beta_far[:, 2, :], bt[:, 3, :], far[:, 2, :])
                b.wait(act, "g_sig")
                b.wait(pool, "ctx")
                mul("gate", gate[nxt.par][:, :], gate_in[:, :], g_sig)
            if chain:
                q_times_s(4)
            if pre:
                mul("beta_gam", beta_gam[nxt.par][:, :], beta, gam[nxt.par][:, :])
            if chain:
                q_times_s(5)
            if chain:
                q_times_s(6)
            if chain:
                q_times_s(7)
            if b.kind == POST_ONLY and not b.dry:
                to_sorted(b.eng, 3 * NCH + TW, NT_A)

        def dve_body(b):
            w = b.win
            pre, chain, post = HAS_PRE[b.kind], HAS_CHAIN[b.kind], HAS_POST[b.kind]
            nxt, prv = w.shift(1), w.shift(-1)
            v = nc.vector
            HB = NB // 2

            def r3(bank):
                return bank[:, 0:3 * NN].rearrange("p (s n) -> p s n", s=3)

            def half_chunk(c, h):
                bs = slice(h * HB, (h + 1) * HB)
                kr, dl = k_rep[w.par], slot_chunk(delta[w.par], c)[:, :, bs]
                s_in, s_out = S[c % NS][:, bs, :], S[(c + 1) % NS][:, bs, :]
                up, ks_h, tri_h, de = upd[:, bs, :, :], ks[:, :, bs], tri[:, :, bs], d_end[:, :, bs]
                n = C * HB * DH
                at = h * HB * DH * (C + 1)
                flat = upd[:, :, :, :].rearrange("p b d s -> p (b d s)")[:, at:at + n]
                prod = flat.rearrange("p (j b d) -> p j b d", j=C, b=HB)

                def rep(order):
                    return k_rep[w.par][:, :, :].rearrange("p d (b c j) -> p c d b j", c=NCH, j=C)[:, c, :, bs, :] \
                        .rearrange(f"p d b j -> p {order}")
                yield "k_prod", lambda: v.tensor_tensor(
                    prod, s_in.unsqueeze(1).to_broadcast([P, C, HB, DH]), rep("j b d"), ALU.mult)
                yield "k_sum", lambda: v.tensor_reduce(ks_h, prod, AX, ALU.add)
                yield "decay", lambda: v.tensor_tensor(
                    up[:, :, :, C], s_in,
                    chunk_jb(gam[w.par][:, :], c)[:, C - 1, bs].unsqueeze(2).to_broadcast([P, HB, DH]), ALU.mult)
                yield "k_gam", lambda: v.tensor_tensor(ks_h, ks_h, chunk_jb(beta_gam[w.par][:, :], c)[:, :, bs], ALU.mult)
                yield "rhs", lambda: v.tensor_tensor(dl, chunk_jb(beta_v[w.par][:, :], c)[:, :, bs], ks_h, ALU.subtract)
                for s in range(C - 1):
                    m = C - 1 - s
                    a = slot_chunk(akk[w.par], c)[:, s:s + C * (m - 1) + 1:C, bs]
                    yield f"tri{s}", lambda: v.tensor_tensor(
                        tri_h[:, 0:m, :], a, dl[:, s:s + 1, :].to_broadcast([P, m, HB]), ALU.mult)
                    yield f"sub{s}", lambda: v.tensor_tensor(
                        dl[:, s + 1:C, :], dl[:, s + 1:C, :], tri_h[:, 0:m, :], ALU.subtract)
                yield "d_end", lambda: v.tensor_tensor(de, dl, slot_chunk(to_end[w.par], c)[:, :, bs], ALU.mult)
                yield "upd", lambda: v.tensor_tensor(
                    up[:, :, :, 0:C], rep("b d j"),
                    de.rearrange("p j b -> p b j").unsqueeze(2).to_broadcast([P, HB, DH, C]), ALU.mult)
                yield "S", lambda: v.tensor_reduce(s_out, up, AX, ALU.add)

            def chunk(c):
                if c == 0:
                    if not b.dry:
                        b.dma(s_krep, w)
                    b.wait(pool, "beta_gam", back=1)
                    b.wait(act, "to_end0", back=1)
                    b.wait(dve, "akk_far", back=1)
                before, done = w.w * NCH + c, w.w * NCH + c + 1
                if not isinstance(before, int) and not b.dry:
                    before, done = b.eng.to_reg(before), b.eng.to_reg(done)
                for k, pair in enumerate(zip(half_chunk(c, 0), half_chunk(c, 1))):
                    for h, (name, ins) in enumerate(pair):
                        assert name == links[k]
                        if name == "S":
                            b.wait(pool, f"q_prod{(c + 1 - NS) % NCH}", back=0 if c + 1 >= NS else 1)
                        if b.dry:
                            continue
                        if k:
                            b.eng.wait_ge(s_link[links[k - 1], h], done)
                        elif not isinstance(before, int) or before > 0:
                            b.eng.wait_ge(s_link["S", h], before)
                        ins().then_inc(s_link[name, h], 1)

            if chain:
                chunk(0)
                chunk(1)
                chunk(2)
                chunk(3)
            if post:
                b.wait(act, "rms_r")
                b.step("y_n", lambda: v.tensor_tensor(y_n, y_ps[prv.par], y_sq[:, :], ALU.mult))
            if pre:
                b.wait(act, "beta")
                b.wait(pe, "v")
                b.step("beta_v", lambda: v.tensor_tensor(beta_v[nxt.par][:, :], zbg_ps[:, 0, :], beta, ALU.mult))
            if chain:
                chunk(4)
            if post:
                b.wait(pe, "attn")
                for i in range(TW):
                    b.step(f"stats{i}", lambda: v.bn_stats(stats[:, i, :], post_ps[:, i * D:(i + 1) * D]))
                b.own()
                b.step("settle", lambda: v.tensor_copy(settle[:, :], ones[:, 0:1]))
                for i in range(TW):
                    b.step(f"mv{i}", lambda: v.bn_aggr(mv[:, i, :], stats[:, i, :]))
            if chain:
                chunk(5)
            if pre:
                aq = aqk[nxt.par]
                b.wait(pe, "qk_near")
                b.step("aqk_near", lambda: v.tensor_tensor(aq[:, 4:7, :], r3(zbg_ps[:, 1, :]), slots(alpha)[:, 1:4, :],
                                                           ALU.mult))
                b.wait(pe, "qk_far")
                b.step("aqk_far", lambda: v.tensor_tensor(aq[:, 7:10, :], r3(zbg_ps[:, 2, :]), far[:, :, :], ALU.mult))
            if post:
                b.wait(act, "ln_r")
                b.step("ln_shift", lambda: v.scalar_tensor_tensor(shift[:, :], mv[:, :, 0], -1.0, rstd[:, :],
                                                                  ALU.mult, ALU.mult))
            if chain:
                chunk(6)
            if pre:
                ak = akk[nxt.par]
                near, away = r3(kq_ps[:, 0, :]), r3(kq_ps[:, 1, :])
                b.wait(pe, "kk_near")
                b.wait(pool, "beta_far2")
                b.step("akk_near", lambda: v.tensor_tensor(ak[:, 0:3, :], near, beta_near, ALU.mult))
                b.wait(pe, "kk_far")
                b.step("akk_far2", lambda: v.tensor_tensor(ak[:, 8, :], away[:, 2, :], beta_far[:, 2, :], ALU.mult))
                b.step("akk_far", lambda: v.tensor_tensor(ak[:, 4:6, :], away[:, 0:2, :], beta_far[:, 0:2, :], ALU.mult))
            if chain:
                chunk(7)

        def sp_body(b):
            w = b.win
            pre, chain, post = HAS_PRE[b.kind], HAS_CHAIN[b.kind], HAS_POST[b.kind]
            nxt, prv, far2 = w.shift(1), w.shift(-1), w.shift(2)
            e = b.eng
            if chain:
                if not (isinstance(w.w, int) and w.w + 2 >= NW):
                    b.wait(pe, "v", back=1)
                    e.dma_start(x_ct[w.par][:, :], t["x_ct"][:, bass.ds(far2.w, 1), :].rearrange("p o n -> p (o n)")) \
                        .then_inc(s_xct[w.par], 16)
            if pre:
                if not (isinstance(w.w, int) and w.w <= 0):
                    b.dma(s_krep, prv)
                    b.dma(s_qrep, prv)
                b.wait(pool, "kq_n")
                e.dma_start(t["k_dram"][nxt.par], k_s).then_inc(s_kout, 16)
                b.wait(pool, "q_gam")
                e.dma_start(t["q_dram"][nxt.par], q_scaled).then_inc(s_qout, 16)
                for name, dst, s_out, s_rep in (("k_dram", k_rep, s_kout, s_krep), ("q_dram", q_rep, s_qout, s_qrep)):
                    b.dma1(s_out, nxt)
                    src = t[name][nxt.par].rearrange("(h d) n -> h (d n)", d=DH).unsqueeze(1).to_broadcast([H, DH, DH * WN])
                    e.dma_start(dst[nxt.par][:, :, :].rearrange("p d n -> p (d n)"), src).then_inc(s_rep[nxt.par], 16)
            if chain:
                b.wait(pe, "res")
                e.dma_start(x_tc[:, :], t["x_tc"][bass.ds(w.w, 1), :, :].rearrange("o p n -> (o p) n")) \
                    .then_inc(s_xtc[w.par], 16)

        def windows(steps, eng, body, setup):
            def run(kind, win):
                body(Body(steps, eng, kind, win, False))
            setup(eng)
            run(PRE_ONLY, Win(-1, 1))
            run(FIRST, Win(0, 0))
            run(FULL, Win(0, 1))
            with eng.Fori(1, NW // 2 - 1) as i:
                run(FULL, Win(i, 0))
                run(FULL, Win(i, 1))
            run(FULL, Win(NW // 2 - 1, 0))
            before_last(eng)
            run(LAST, Win(NW // 2 - 1, 1))
            run(POST_ONLY, Win(NW // 2, 0))

        for steps, body in ((pe, pe_body), (act, act_body), (pool, pool_body), (dve, dve_body)):
            for kind in range(5):
                body(Body(steps, None, kind, Win(0, 0), True))

        n_const = 16 * (len(t["consts"]) + 4)
        n_setup = 9
        tiles = dict(w_q=w_proj[:, 0, :], w_k=w_proj[:, 1, :], w_v=w_proj[:, 2, :], w_g=w_proj[:, 3, :],
                     w_b=w_proj[:, 4, :], w_a=w_a[:, :], w_o=w_o[:, :], w_r=w_r[:, :], ident=ident[:, :],
                     heads=heads[:, :], heads_q=heads_q[:, :], heads_mean=heads_mean[:, :], below=below[:, :], ones=ones[:, :],
                     iota_e=iota_e[:, :], token=token,
                     none=no_token[:, D:D + 1])

        def load_constants(e, half):
            for name, src in list(t["consts"].items())[half::2]:
                e.dma_start(tiles[name], src).then_inc(s_const, 16)

        @block.sync
        def _(eng):
            def setup(e):
                load_constants(e, 0)
                for n in range(2):
                    e.dma_start(x_ct[n][:, :], t["x_ct"][:, n, :]).then_inc(s_xct[n], 16)
                e.dma_start(dt_in[:, :], t["dt_bias"].rearrange("(o h) -> o h", o=1)).then_inc(s_const, 16)
                e.dma_start(neg_a[:, :], t["A_log"].rearrange("(h o) -> h o", o=1).unsqueeze(1)
                            .to_broadcast([H, DH, 1])).then_inc(s_const, 16)
                e.dma_start(norm_w[:, :], t["norm_w"].rearrange("(d o) -> d o", o=1).unsqueeze(0)
                            .to_broadcast([H, DH, 1])).then_inc(s_const, 16)
                e.dma_start(bias_o[:, :], t["bo"].rearrange("(o n) -> o n", o=1)).then_inc(s_const, 16)
                e.wait_ge(s_setup, n_setup)
                e.dma_start(t["x_sorted"][E * REGION:E * (REGION + P), :].rearrange("(m p) d -> p m d", p=P),
                            no_token[:, :].unsqueeze(1).to_broadcast([P, E, D + 1])).then_inc(s_pad, 16)
            windows(Steps(None), eng, sp_body, setup)
            finish_sync(eng)


        @block.tensor
        def _(eng):
            def setup(e):
                e.wait_ge(s_const, n_const)
                e.wait_ge(s_setup, n_setup)
            windows(pe, eng, pe_body, setup)
            finish_pe(eng)

        @block.scalar
        def _(eng):
            def setup(e):
                load_constants(e, 1)
                e.wait_ge(s_const, n_const)
                e.wait_ge(s_setup, n_setup)
                nc.scalar.preload_act_table_set("natural_log_exp_and_others")
                nc.scalar.activation(neg_a[:, :], neg_a[:, :], ACT.Exp).then_inc(s_neg_a, 1)
                e.wait_ge(s_neg_a, 1)
                nc.scalar.mul(neg_a[:, :], neg_a[:, :], -1.0).then_inc(s_neg_a, 1)
                e.wait_ge(s_neg_a, 2)
            windows(act, eng, act_body, setup)
            finish_act(eng)

        @block.gpsimd
        def _(eng):
            def setup(e):
                e.wait_ge(s_setup, n_setup)
            windows(pool, eng, pool_body, setup)
            finish_pool(eng)

        @block.vector
        def _(eng):
            def setup(e):
                nc.vector.memset(S[0][:, :, :], 0.0).then_inc(s_setup, 1)
                for n in range(2):
                    nc.vector.memset(to_end[n][:, C - 1, :], 1.0).then_inc(s_setup, 1)
                nc.vector.memset(no_token[:, 0:D], 0.0).then_inc(s_setup, 1)
                nc.vector.memset(rms_eps[:, :], RMS_EPS).then_inc(s_setup, 1)
                e.wait_ge(s_const, n_const)
                nc.vector.memset(ln_eps[:, :], LN_EPS).then_inc(s_setup, 1)
                nc.vector.tensor_copy(x1_all[:, :, D], token).then_inc(s_setup, 1)
                for row, src in ((w_proj[:, 5, :], w_a[:, :]), (dt_row[:, :], dt_in[:, :])):
                    nc.vector.tensor_scalar(row.rearrange("p (h d) -> p h d", d=DH),
                                            src.unsqueeze(2).to_broadcast([src.shape[0], H, DH]), -1.0, None,
                                            ALU.mult).then_inc(s_setup, 1)
                e.wait_ge(s_setup, n_setup)
            windows(dve, eng, dve_body, setup)
            finish_dve(eng)


def kernel(**inputs):
    import numpy as _np
    import concourse.bacc as _bacc
    from concourse import mybir as _mybir
    from concourse.bass_utils import run_bass_kernel_spmd as _run

    a = {k: _np.ascontiguousarray(v) for k, v in inputs.items()}
    f = _np.float32
    x = a["L0_attn_x"]
    chan = _np.arange(P)
    same_head = (chan[:, None] // DH == chan[None, :] // DH).astype(f)
    down = _np.zeros((E, IC * P, D), a["L0_ffn_down_w"].dtype)
    down[:, :I, :] = a["L0_ffn_down_w"].transpose(0, 2, 1)
    arrays = {
        "x_ct": x.reshape(NB, NW, T, D).transpose(3, 1, 0, 2).reshape(D, NW, WN),
        "x_tc": x.reshape(TW, NB // TW, NW, T, D).transpose(2, 1, 3, 0, 4).reshape(NW, P, TW * D),
        "w_q": a["L0_attn_Wq"].T, "w_k": a["L0_attn_Wk"].T, "w_v": a["L0_attn_Wv"].T,
        "w_g": a["L0_attn_Wg"].T, "w_b": a["L0_attn_Wb"].T, "w_a": a["L0_attn_Wa"].T,
        "w_o": a["L0_attn_Wo"].T, "w_r": a["L0_ffn_router_w"].T,
        "dt_bias": a["L0_attn_dt_bias"], "A_log": a["L0_attn_A_log"], "norm_w": a["L0_attn_norm_w"],
        "bo": a["L0_attn_bo"],
        "gate_w": a["L0_ffn_gate_w"].transpose(2, 0, 1), "up_w": a["L0_ffn_up_w"].transpose(2, 0, 1),
        "down_w": down.reshape(E, IC, P, D).transpose(2, 1, 0, 3),
        "ident": _np.eye(P, dtype=f), "heads": same_head, "heads_q": same_head * f(DH), "heads_mean": same_head / f(DH),
        "below": (chan[:, None] < chan[None, :]).astype(f), "ones": _np.ones((P, P), f),
        "iota_e": _np.tile(_np.arange(E, dtype=f), (P, 1)), "iota_t": _np.arange(MT, dtype=f)[None, :],
        "token": (_np.arange(NT)[None, :] * P + chan[:, None]).astype(f), "none": (NT * P + chan[:, None]).astype(f),
    }
    arrays = {k: _np.ascontiguousarray(v) for k, v in arrays.items()}
    nc = _bacc.Bacc("TRN2", target_bir_lowering=False, num_devices=1)
    dram = {k: nc.dram_tensor(f"in_{k}", v.shape, _mybir.dt.from_np(v.dtype), kind="ExternalInput").ap()
            for k, v in arrays.items()}
    names = ("w_q", "w_k", "w_v", "w_g", "w_b", "w_a", "w_o", "w_r", "ident", "heads", "heads_q", "heads_mean",
             "below", "ones",
             "iota_e", "token", "none")
    dram["consts"] = {k: dram[k] for k in names}
    dram["k_dram"] = [nc.dram_tensor(f"k_dram{n}", (P, WN), F32, kind="Internal").ap() for n in range(2)]
    dram["q_dram"] = [nc.dram_tensor(f"q_dram{n}", (P, WN), F32, kind="Internal").ap() for n in range(2)]
    dram["x_sorted"] = nc.dram_tensor("x_sorted", (E * (REGION + P), D + 1), F32, kind="Internal").ap()
    dram["out"] = nc.dram_tensor("out_0", (NT * P, D), F32, kind="ExternalOutput").ap()
    block_kernel(nc, dram)
    r = _run(nc, [{f"in_{k}": v for k, v in arrays.items()}], core_ids=[0])
    y = r.results[0]["out_0"].reshape(NW, TW, NB // TW, T, D)
    return _np.ascontiguousarray(y.transpose(1, 2, 0, 3, 4).reshape(NB, L, D))
```
